# Optimizing a Trainium2 kernel written in Bass

```python
import numpy as np
import jax
import jax.numpy as jnp

def _softmax(x, axis=-1):
    return jax.nn.softmax(x, axis=axis)

def _gelu(x):
    return jax.nn.gelu(x, approximate=True)

def _silu(x):
    return jax.nn.silu(x)

def _sigmoid(x):
    return jax.nn.sigmoid(x)

def _layernorm(x, axis=-1, eps=1e-05):
    m = jnp.mean(x, axis=axis, keepdims=True)
    v = jnp.var(x, axis=axis, keepdims=True)
    return (x - m) / jnp.sqrt(v + eps)

def _scatter_add(tgt, idx, src, axis=0):
    return tgt.at[idx].add(src)

def _segment_sum(src, seg, n):
    return jax.ops.segment_sum(src, seg, n)
kernel_name = 'mk_adaln_d1_jaxref_r4_969ac7'

def setup_inputs(seed: int=0):
    np.random.seed(seed)
    _w = jnp.asarray

    def _L0_attn_setup():
        import jax, jax.numpy as jnp
        import numpy as np
        HIDDEN = 512
        NUM_HEADS = 16
        HEAD_DIM = HIDDEN // NUM_HEADS
        RANK = 64
        BATCH = 1
        SEQ = 512
        key = jax.random.key(seed)
        k1, k2, k3, k4, k5 = jax.random.split(key, 5)
        s_in = 0.02
        return {'hidden_states': jax.random.normal(k1, (BATCH, SEQ, HIDDEN), jnp.float32), 'Wq': jax.random.normal(k2, (RANK, HIDDEN), jnp.float32) * s_in, 'Wk': jax.random.normal(k3, (RANK, HIDDEN), jnp.float32) * s_in, 'Wv': jax.random.normal(k4, (HIDDEN, HIDDEN), jnp.float32) * s_in, 'Wo': jax.random.normal(k5, (HIDDEN, HIDDEN), jnp.float32) * s_in}
    _L0_attn_in = _L0_attn_setup()

    def _L0_ffn_setup():
        import math
        import jax, jax.numpy as jnp
        import numpy as np
        DIM = 512
        RANK = 8
        B, T = (4, 1024)

        def _orthogonal(key, n):
            a = jax.random.normal(key, (n, n), dtype=jnp.float32)
            q, r = jnp.linalg.qr(a)
            q = q * jnp.sign(jnp.diagonal(r))[None, :]
            return q
        key = jax.random.key(seed)
        kx, kf = jax.random.split(key)
        x = jax.random.normal(kx, (B, T, DIM), dtype=jnp.float32)
        fkeys = jax.random.split(kf, RANK)
        factors = jnp.stack([_orthogonal(fkeys[r], DIM) * (r + 1) ** (-0.5) for r in range(RANK)])
        bias = jnp.zeros((DIM,), dtype=jnp.float32)
        return {'x': x, 'factors': factors, 'bias': bias}
    _L0_ffn_in = _L0_ffn_setup()
    _L0_c = _w((lambda *s: np.random.randn(*s).astype(np.float32) * 0.05)(4, 512))
    _L0_wmod = _w((lambda *s: np.random.randn(*s).astype(np.float32) * 0.05)(512, 6 * 512) * 512 ** (-0.5))
    _d = {'L0_attn_hidden_states': _L0_attn_in['hidden_states'], 'L0_attn_Wq': _L0_attn_in['Wq'], 'L0_attn_Wk': _L0_attn_in['Wk'], 'L0_attn_Wv': _L0_attn_in['Wv'], 'L0_attn_Wo': _L0_attn_in['Wo'], 'L0_ffn_factors': _L0_ffn_in['factors'], 'L0_ffn_bias': _L0_ffn_in['bias'], 'L0_c': _L0_c, 'L0_wmod': _L0_wmod}
    _x0 = _d['L0_attn_hidden_states']
    _d['L0_attn_hidden_states'] = jax.random.normal(jax.random.fold_in(jax.random.key(seed), 1), (4, 1024, 512), dtype=_x0.dtype)
    del _x0
    return _d

def reference(L0_attn_hidden_states, L0_attn_Wq, L0_attn_Wk, L0_attn_Wv, L0_attn_Wo, L0_ffn_factors, L0_ffn_bias, L0_c, L0_wmod):

    def _L0_attn_ref(hidden_states, Wq, Wk, Wv, Wo):
        import jax, jax.numpy as jnp
        import numpy as np
        HIDDEN = 512
        NUM_HEADS = 16
        HEAD_DIM = HIDDEN // NUM_HEADS
        RANK = 64
        BATCH = 1
        SEQ = 512
        b, s, _ = hidden_states.shape
        qf = hidden_states @ Wq.T
        kf = hidden_states @ Wk.T
        head_f = jnp.ones((NUM_HEADS, RANK), hidden_states.dtype)
        scores = jnp.einsum('hr,bir,bjr->bhij', head_f, qf, kf)
        attn = jax.nn.softmax(scores.astype(jnp.float32), axis=-1).astype(hidden_states.dtype)
        v = (hidden_states @ Wv.T).reshape(b, s, NUM_HEADS, HEAD_DIM).transpose(0, 2, 1, 3)
        out = jnp.einsum('bhij,bhjd->bhid', attn, v)
        out = out.transpose(0, 2, 1, 3).reshape(b, s, HIDDEN)
        return out @ Wo.T

    def _L0_ffn_ref(x, factors, bias):
        import math
        import jax, jax.numpy as jnp
        import numpy as np
        DIM = 512
        RANK = 8
        B, T = (4, 1024)

        def _orthogonal(key, n):
            a = jax.random.normal(key, (n, n), dtype=jnp.float32)
            q, r = jnp.linalg.qr(a)
            q = q * jnp.sign(jnp.diagonal(r))[None, :]
            return q
        rank = factors.shape[0]
        mixed = jnp.einsum('btd,rde->bte', x, factors)
        mixed = mixed / math.sqrt(rank) + bias
        return mixed
    x = L0_attn_hidden_states
    mod = (_silu(L0_c) @ L0_wmod).reshape(L0_c.shape[0], 6, 1, -1)
    sa, ca, ga, sb, cb, gb = (mod[:, 0], mod[:, 1], mod[:, 2], mod[:, 3], mod[:, 4], mod[:, 5])
    ga = (2 * (ga >= 0) - 1) * jnp.maximum(jnp.abs(ga), 0.25)
    gb = (2 * (gb >= 0) - 1) * jnp.maximum(jnp.abs(gb), 0.25)
    h = _layernorm(x, axis=-1) * (1 + ca) + sa
    x = x + ga * _L0_attn_ref(h, L0_attn_Wq, L0_attn_Wk, L0_attn_Wv, L0_attn_Wo)
    h = _layernorm(x, axis=-1) * (1 + cb) + sb
    x = x + gb * _L0_ffn_ref(h, L0_ffn_factors, L0_ffn_bias)
    return x

_drawn_inputs = setup_inputs


def setup_inputs(seed=0):
    import zlib

    import numpy as np

    out = dict(_drawn_inputs(seed))
    spreads = {'L0_ffn_bias': (0.0, 0.877)}
    factors = {'L0_attn_Wq': 7.96, 'L0_attn_Wk': 7.449, 'L0_attn_Wv': 7.243, 'L0_attn_Wo': 7.234}
    for name, (base, spread) in spreads.items():
        noise = np.random.default_rng([zlib.crc32(name.encode()), seed]).standard_normal(out[name].shape)
        drawn = base * np.exp(spread * noise) if base else spread * noise
        out[name] = jnp.asarray(drawn.astype(out[name].dtype))
    for name, factor in factors.items():
        out[name] = (out[name] * factor).astype(out[name].dtype)
    return out
```

```python
from contextlib import ExitStack

import concourse.bass as bass
from concourse import mybir

F32 = mybir.dt.float32
F32R = mybir.dt.float32r
ACT = mybir.ActivationFunctionType
ALU = mybir.AluOpType
AX_X = mybir.AxisListType.X

P = 128
EPS = 1e-5
GATE_STEPS = 4
GATE_FLOOR = 0.25
SA, CA, GA, SB, CB, GB = range(6)


def adaln_block(nc, x, wqk_t, wv, wo_t, factors, bias, c_t, wmod, out):
    tokens, D = x.shape
    B = c_t.shape[1] // (D // P)
    C = D // P
    TB = tokens // B // P
    T = tokens // P
    PAIRS, PB = T // 2, TB // 2
    KEYS = TB * P
    R = wqk_t.shape[1] // 2
    NF = factors.shape[0]
    HALF = TB // 2
    NS = 3
    FSCALE = 1.0 / float(NF) ** 0.5
    assert (P, D, R, C, TB, B) == (128, 512, 64, 4, 8, 4) and KEYS == 2 * D

    x_pairs = x.rearrange("(g u p) d -> g p u d", u=2, p=P)
    out_pairs = out.rearrange("(g u p) d -> g p u d", u=2, p=P)
    gate_rows = nc.dram_tensor("gate_rows", [2, B, D], F32, kind="Internal").ap()

    with ExitStack() as ctx:
        def sb(name, shape, dt=F32, stack=ctx):
            return stack.enter_context(nc.sbuf_tensor(name, shape, dt))

        def bank(name, columns=D):
            return ctx.enter_context(nc.psum_tensor(name, [P, columns], F32))

        def sem(name):
            return ctx.enter_context(nc.semaphore(name))

        ident = sb("ident", [P, P])
        c_sb = sb("c_sb", [P, C, B])
        silu_den = sb("silu_den", [P, C, B])
        silu_c = sb("silu_c", [P, C, B])
        mod_t = sb("mod_t", [P, B, 4, C])
        stats1 = sb("stats1", [P, 2, 6])
        stats2 = sb("stats2", [P, 2, 6])
        mv1 = sb("mv1", [P, 2, 2])
        mv2 = sb("mv2", [P, 2, 2])
        ve1 = sb("ve1", [P, 2])
        ve2 = sb("ve2", [P, 2])
        rstd1 = sb("rstd1", [P, 2])
        rstd2 = sb("rstd2", [P, 2])
        nmr1 = sb("nmr1", [P, 2])
        nmr2 = sb("nmr2", [P, 2])
        minus_half = sb("minus_half", [P, 1])
        negmax = sb("negmax", [P, 2])
        rowsum = sb("rowsum", [P, 2])
        rden = sb("rden", [P, 2])
        bias_bc = sb("bias_bc", [P, D])
        wvo_hi = sb("wvo_hi", [P, C, D], F32R)
        wvo_lo = sb("wvo_lo", [P, C, D], F32R)
        wqk_hi = sb("wqk_hi", [P, C, 2 * R], F32R)
        wqk_lo = sb("wqk_lo", [P, C, 2 * R], F32R)
        xn = sb("xn", [P, D])
        h_f = sb("h_f", [P, C, P])
        h_hi = sb("h_hi", [P, C, 2 * P], F32R)
        h_lo = sb("h_lo", [P, C, 2 * P], F32R)
        qk_hi = sb("qk_hi", [P, PB, 2 * P], F32R)
        qk_lo = sb("qk_lo", [P, PB, 2 * P], F32R)
        k_both = sb("k_both", [P, 2 * PB, 2 * P], F32R)
        gates = sb("gates", [P, 2, B, D])
        mod_rows = gates[0:B].rearrange("b a c d -> b (a c) d")

        with ExitStack() as setup:
            sb("under_x", [P, 10, D], F32, setup)
            f_stage = sb("f_stage", [P, NS, 2, D], F32, setup)
            sb("under_v_hi", [P, TB, D], F32, setup)
            wmod_0 = sb("wmod_0", [P, C, 2 * D], F32, setup)
            sb("under_v_lo", [P, TB, D], F32, setup)
            wmod_1 = sb("wmod_1", [P, C, 2 * D], F32, setup)
            wmod_2 = sb("wmod_2", [P, C, 2 * D], F32, setup)
            wqk_raw = sb("wqk_raw", [P, C, 2 * R], F32, setup)
            wv_raw = sb("wv_raw", [P, C, D], F32, setup)
            wo_raw = sb("wo_raw", [P, C, D], F32, setup)
            f_sum = sb("f_sum", [P, C, D], F32, setup)
        wmod_sb = [wmod_0, wmod_1, wmod_2]

        x_ring = sb("x_ring", [P, 2 * TB, D])
        v_hi = sb("v_hi", [P, 2 * TB, D], F32R)
        v_lo = sb("v_lo", [P, 2 * TB, D], F32R)
        pt_hi = sb("pt_hi", [P, TB, P], F32R)
        pt_lo = sb("pt_lo", [P, TB, P], F32R)
        probs = sb("probs", [P, KEYS])
        qs_hi = sb("qs_hi", [P, 2 * P], F32R)
        qs_lo = sb("qs_lo", [P, 2 * P], F32R)
        h2_hi = sb("h2_hi", [P, C, P], F32R)
        h2_lo = sb("h2_lo", [P, C, P], F32R)
        f_hi = sb("f_hi", [P, C, D], F32R)
        f_lo = sb("f_lo", [P, C, D], F32R)
        x2n = sb("x2n", [P, D])
        attn = sb("attn", [P, D])
        ffn = sb("ffn", [P, D])
        h2_f = sb("h2_f", [P, C, P])

        ps_s = bank("ps_s", KEYS)
        ps_t = [bank("ps_t0"), bank("ps_t1")]
        ps_v = bank("ps_v")
        ps_o = bank("ps_o")
        ps_y = bank("ps_y")
        ps_qk = bank("ps_qk")
        mod_banks = [ps_s[:, 0:D], ps_s[:, D:], ps_s[:, 0:D], ps_s[:, D:], ps_o[:], ps_y[:]]
        wvo_banks = [ps_v, ps_o, ps_y, ps_qk]

        c_loaded, wqk_loaded, bias_loaded, wv_loaded, wo_loaded, f0_loaded = (
            sem(n) for n in ("c_loaded", "wqk_loaded", "bias_loaded", "wv_loaded", "wo_loaded", "f0_loaded"))
        wmod_loaded = [sem(f"wmod_loaded{i}") for i in range(3)]
        stage_loaded = [sem(f"stage_loaded{i}") for i in range(NS)]
        x_loaded = sem("x_loaded")
        y_stored = sem("y_stored")
        last_stored = sem("last_stored")
        gates_stored, gates_loaded = sem("gates_stored"), sem("gates_loaded")
        consts_set = sem("consts_set")
        ident_set = sem("ident_set")
        silu_exp, silu_steps = sem("silu_exp"), sem("silu_steps")
        mod_acc = sem("mod_acc")
        rows_done = sem("rows_done")
        mod_tps = sem("mod_tps")
        mod_t_done = sem("mod_t_done")
        wvo_acc, wvo_hi_done, wvo_lo_done = sem("wvo_acc"), sem("wvo_hi_done"), sem("wvo_lo_done")
        wqk_hi_done, wqk_lo_done = sem("wqk_hi_done"), sem("wqk_lo_done")
        f_added, f_hi_done, f_lo_done = sem("f_added"), sem("f_hi_done"), sem("f_lo_done")
        sp_passed, dve_passed, pool_passed = sem("sp_passed"), sem("dve_passed"), sem("pool_passed")
        stats1_done, mv1_done, ve1_done, rstd1_done, nmr1_done = (
            sem(n) for n in ("stats1_done", "mv1_done", "ve1_done", "rstd1_done", "nmr1_done"))
        xn_done, xt_ps, h_f_done, h_hi_done, h_lo_done = (
            sem(n) for n in ("xn_done", "xt_ps", "h_f_done", "h_hi_done", "h_lo_done"))
        v_acc, v_hi_done, v_lo_done = sem("v_acc"), sem("v_hi_done"), sem("v_lo_done")
        qk_acc, qk_hi_done, qk_lo_done, k_hi_done, k_lo_done = (
            sem(n) for n in ("qk_acc", "qk_hi_done", "qk_lo_done", "k_hi_done", "k_lo_done"))
        qs_hi_done, qs_lo_done = sem("qs_hi_done"), sem("qs_lo_done")
        s_acc, max_done, exp_done = sem("s_acc"), sem("max_done"), sem("exp_done")
        pt_ps, pt_hi_done, pt_lo_done, o_acc = (
            sem(n) for n in ("pt_ps", "pt_hi_done", "pt_lo_done", "o_acc"))
        rden_done, attn_done, x1_done = sem("rden_done"), sem("attn_done"), sem("x1_done")
        stats2_done, mv2_done, ve2_done, rstd2_done, nmr2_done = (
            sem(n) for n in ("stats2_done", "mv2_done", "ve2_done", "rstd2_done", "nmr2_done"))
        x2n_done, h2_ps, h2_f_done, h2_hi_done, h2_lo_done = (
            sem(n) for n in ("x2n_done", "h2_ps", "h2_f_done", "h2_hi_done", "h2_lo_done"))
        y_acc, ffn_done, gated_done, y_done = sem("y_acc"), sem("ffn_done"), sem("gated_done"), sem("y_done")

        def wait(eng, semaphore, value):
            if not isinstance(value, int) or value > 0:
                eng.wait_ge(semaphore, value)

        def wait_alone(eng, passed, semaphore, value):
            eng.wait_ge(semaphore, value)
            eng.sem_inc(passed, 1)

        def batch_of(pair):
            return (pair >> 2) & (B - 1)

        def full(ap):
            return ap.bitcast(F32)

        block = ctx.enter_context(nc.Block())

        @block.sync
        def _(sp):
            def load_x(pair):
                if not isinstance(pair, int) or pair > 0:
                    wait_alone(sp, sp_passed, x_loaded, pair * 16)
                slot = (pair & (2 * PB - 1)) * 2
                sp.dma_start(x_ring[:, bass.ds(slot, 2), :], x_pairs[pair]).then_inc(x_loaded, 16)

            def store_pair(pair):
                wait_alone(sp, sp_passed, y_done, 2 * pair + 2)
                if not isinstance(pair, int) or pair > 0:
                    wait_alone(sp, sp_passed, y_stored, pair * 16)
                slot = (pair & (2 * PB - 1)) * 2
                sp.dma_start(out_pairs[pair], x_ring[:, bass.ds(slot, 2), :]).then_inc(y_stored, 16)

            def load_wmod(i):
                sp.dma_start(wmod_sb[i][:], wmod[:, 2 * D * i:2 * D * (i + 1)].rearrange(
                    "(c p) n -> p c n", p=P)).then_inc(wmod_loaded[i], 16)

            sp.dma_start(c_sb[:].rearrange("p c b -> p (c b)"), c_t).then_inc(c_loaded, 16)
            load_wmod(0)
            load_x(0)
            sp.dma_start(wv_raw[:], wv.rearrange("(c p) n -> p c n", p=P)).then_inc(wv_loaded, 16)
            sp.dma_start(wo_raw[:], wo_t.rearrange("(c p) n -> p c n", p=P)).then_inc(wo_loaded, 16)
            sp.dma_start(wqk_raw[:], wqk_t.rearrange("(c p) n -> p c n", p=P)).then_inc(wqk_loaded, 16)
            load_wmod(1)
            load_x(1)
            load_wmod(2)
            load_x(2)
            sp.dma_start(bias_bc[:], bias.partition_broadcast(P)).then_inc(bias_loaded, 16)
            sp.dma_start(f_sum[:], factors[0].rearrange("(c p) n -> p c n", p=P)).then_inc(f0_loaded, 16)
            load_x(3)
            load_x(4)
            for i in range(2 * (NF - 1)):
                wait(sp, f_added, i - NS + 1)
                src = factors[1 + i // 2].rearrange("(h c p) n -> h p c n", h=2, p=P)[i % 2]
                sp.dma_start(f_stage[:, i % NS], src).then_inc(stage_loaded[i % NS], 16)
            sp.wait_ge(f_added, 2 * (NF - 1))
            for pair in range(5, 2 * PB):
                load_x(pair)
            def turn_over(pair):
                store_pair(pair)
                wait_alone(sp, sp_passed, y_stored, pair * 16 + 16)
                load_x(pair + 2 * PB)

            turn_over(0)
            with sp.Fori(1, PAIRS - 2 * PB) as pair:
                turn_over(pair)
            with sp.Fori(PAIRS - 2 * PB, PAIRS - 1) as pair:
                store_pair(pair)
            last = PAIRS - 1
            for u in range(2):
                sp.wait_ge(y_done, 2 * last + u + 1)
                sp.dma_start(out_pairs[last][:, u], x_ring[:, 2 * TB - 2 + u, :]).then_inc(last_stored, 16)
            sp.wait_ge(y_stored, last * 16)
            sp.wait_ge(last_stored, 32)

        @block.tensor
        def _(pe):
            def three(acc, a, b, first, last):
                (a_hi, a_lo), (b_hi, b_lo) = a, b
                nc.tensor.matmul(acc, a_hi, b_lo, start=first, stop=False)
                nc.tensor.matmul(acc, a_lo, b_hi, start=False, stop=False)
                return nc.tensor.matmul(acc, a_hi, b_hi, start=False, stop=last)

            def transposes(acc, source, n, base=0):
                for i in range(n):
                    last = nc.tensor.transpose(acc[:, P * i:P * (i + 1)],
                                               source[:, P * (base + i):P * (base + i + 1)], ident[:])
                return last

            def modulation(v):
                pe.wait_ge(wmod_loaded[v // 2], 16)
                for k in range(C):
                    last = nc.tensor.matmul(mod_banks[v][0:B, :], silu_c[:, k, :],
                                            wmod_sb[v // 2][:, k, D * (v % 2):D * (v % 2 + 1)],
                                            start=(k == 0), stop=(k == C - 1))
                last.then_inc(mod_acc, 1)

            def modulation_columns(vectors):
                for i, v in enumerate(vectors):
                    for k in range(C):
                        at = (i * C + k) * B
                        last = nc.tensor.transpose(ps_t[0][:, at:at + B], mod_rows[:, v, P * k:P * (k + 1)],
                                                   ident[0:B, 0:B])
                last.then_inc(mod_tps, 1)

            def transpose_x(q):
                pe.wait_ge(xn_done, q + 1)
                wait(pe, h_f_done, q)
                transposes(ps_t[1], xn, C).then_inc(xt_ps, 1)

            def project_values(q, u):
                pe.wait_ge(h_lo_done, q + 1)
                wait(pe, v_lo_done, q)
                for k in range(C):
                    h = [part[:, k, P * u:P * (u + 1)] for part in (h_hi, h_lo)]
                    last = three(ps_v[:], h, (wvo_hi[:, k, :], wvo_lo[:, k, :]), k == 0, k == C - 1)
                last.then_inc(v_acc, 1)

            def project_qk(pair):
                wait(pe, qk_lo_done, pair)
                for k in range(C):
                    last = three(ps_qk[:, 0:2 * P], (wqk_hi[:, k, :], wqk_lo[:, k, :]),
                                 (h_hi[:, k, :], h_lo[:, k, :]), k == 0, k == C - 1)
                last.then_inc(qk_acc, 1)

            def scores(t, u, pair):
                pe.wait_ge(qs_hi_done, pair + 1)
                pe.wait_ge(qs_lo_done, pair + 1)
                pe.wait_ge(k_hi_done, (pair >> 2) * PB + PB)
                pe.wait_ge(k_lo_done, (pair >> 2) * PB + PB)
                wait(pe, exp_done, t)
                first = ((pair >> 2) & 1) * PB
                for n in range(2):
                    keys = k_both[:, bass.ds(first + 2 * n, 2), :]
                    acc = ps_s[:, D * n:D * (n + 1)]
                    nc.tensor.matmul(acc, qs_lo[:, P * u:P * (u + 1)], keys, start=True, stop=False)
                    last = nc.tensor.matmul(acc, qs_hi[:, P * u:P * (u + 1)], keys, start=False, stop=True)
                last.then_inc(s_acc, 1)

            def transpose_probs(t, prep):
                pe.wait_ge(exp_done, t + 1)
                wait(pe, h2_f_done, t - 1)
                transposes(ps_t[0], probs, HALF).then_inc(pt_ps, 1)
                if prep:
                    pe.wait_ge(h_f_done, t + TB + 1)
                wait(pe, pt_lo_done, 2 * t)
                transposes(ps_t[1], probs, HALF, HALF).then_inc(pt_ps, 1)

            def transpose_h2(t):
                pe.wait_ge(x2n_done, t + 1)
                pe.wait_ge(pt_lo_done, 2 * t + 3)
                transposes(ps_t[0], x2n, C).then_inc(h2_ps, 1)

            def attend(t, g):
                pe.wait_ge(v_lo_done, (g >> 2) * TB + TB)
                wait(pe, attn_done, t)
                first = ((g >> 2) & 1) * TB
                for j in range(TB):
                    if j % HALF == 0:
                        pe.wait_ge(pt_lo_done, 2 * t + 1 + j // HALF)
                    v = [part[:, first + j, :] for part in (v_hi, v_lo)]
                    last = three(ps_o[:], (pt_hi[:, j, :], pt_lo[:, j, :]), v, j == 0, j == TB - 1)
                last.then_inc(o_acc, 1)

            def feed_forward(t):
                pe.wait_ge(h2_lo_done, t + 1)
                wait(pe, ffn_done, t)
                for k in range(C):
                    last = three(ps_y[:], (h2_hi[:, k, :], h2_lo[:, k, :]),
                                 (f_hi[:, k, :], f_lo[:, k, :]), k == 0, k == C - 1)
                last.then_inc(y_acc, 1)

            def step(g, u, prep=True, next_x=True, following=True, before=True):
                t = 2 * g + u
                transpose_probs(t, prep)
                if prep:
                    project_values(t + TB, u)
                    if u:
                        project_qk(g + PB)
                if following:
                    scores(t + 1, 1 - u, g + u)
                if before:
                    transpose_h2(t - 1)
                if next_x:
                    pe.wait_ge(pt_lo_done, 2 * t + 2)
                    transpose_x(t + TB + 1)
                attend(t, g)
                if before:
                    feed_forward(t - 1)

            pe.wait_ge(silu_steps, 3)
            modulation(SA)
            modulation(CA)
            pe.wait_ge(ident_set, 2)
            pe.wait_ge(rows_done, 2)
            modulation_columns((SA, CA))
            pe.wait_ge(wv_loaded, 16)
            pe.wait_ge(wo_loaded, 16)
            for m in range(C):
                for k in range(C):
                    last = nc.tensor.matmul(wvo_banks[m][:], wv_raw[:, k, P * m:P * (m + 1)], wo_raw[:, k, :],
                                            start=(k == 0), stop=(k == C - 1))
                last.then_inc(wvo_acc, 1)
            modulation(GA)
            modulation(SB)
            pe.wait_ge(wvo_lo_done, C)
            modulation(CB)
            modulation(GB)
            pe.wait_ge(mod_t_done, 2)
            pe.wait_ge(rows_done, 4 + GATE_STEPS)
            modulation_columns((SB, CB))
            pe.wait_ge(rows_done, 4 + 2 * GATE_STEPS)
            pe.wait_ge(wqk_lo_done, 1)
            transpose_x(0)

            def prep_pair(pair):
                for u in range(2):
                    transpose_x(2 * pair + u + 1)
                    project_values(2 * pair + u, u)
                    if u:
                        project_qk(pair)

            prep_pair(0)
            with pe.Fori(1, PB) as pair:
                prep_pair(pair)
            scores(0, 0, 0)
            step(0, 0, before=False)
            pe.wait_ge(f_hi_done, C)
            pe.wait_ge(f_lo_done, C)
            step(0, 1)
            with pe.Fori(1, PAIRS - PB - 1) as g:
                for u in range(2):
                    step(g, u)
            step(PAIRS - PB - 1, 0)
            step(PAIRS - PB - 1, 1, next_x=False)
            with pe.Fori(PAIRS - PB, PAIRS - 1) as g:
                for u in range(2):
                    step(g, u, prep=False, next_x=False)
            step(PAIRS - 1, 0, prep=False, next_x=False)
            step(PAIRS - 1, 1, prep=False, next_x=False, following=False)
            pe.wait_ge(x2n_done, T)
            transposes(ps_t[0], x2n, C).then_inc(h2_ps, 1)
            feed_forward(T - 1)

        @block.scalar
        def _(act):
            def rounded(to, source):
                return nc.scalar.activation(to, source, ACT.Identity)

            def modulate(to, source, b, v):
                for k in range(C):
                    last = nc.scalar.activation(to[:, k, :], source[:, P * k:P * (k + 1)], ACT.Identity,
                                                scale=mod_t[:, b, v + 1, k:k + 1], bias=mod_t[:, b, v, k:k + 1])
                return last

            def normalize_x(q, u):
                act.wait_ge(nmr1_done, q + 1)
                wait(act, xt_ps, q)
                nc.scalar.activation(xn[:], x_ring[:, q & (2 * TB - 1), :], ACT.Identity,
                                     scale=rstd1[:, u:u + 1], bias=nmr1[:, u:u + 1]).then_inc(xn_done, 1)

            def modulate_x(q, b):
                act.wait_ge(xt_ps, q + 1)
                wait(act, h_lo_done, q)
                modulate(h_f, ps_t[1], b, 0).then_inc(h_f_done, 1)

            def values(q):
                act.wait_ge(v_acc, q + 1)
                rounded(v_hi[:, q & (2 * TB - 1), :], ps_v[:]).then_inc(v_hi_done, 1)

            def qk(pair):
                act.wait_ge(qk_acc, pair + 1)
                rounded(qk_hi[:, pair & (PB - 1), :], ps_qk[:, 0:2 * P]).then_inc(qk_hi_done, 1)
                rounded(k_both[0:R, pair & (2 * PB - 1), :], ps_qk[R:2 * R, 0:2 * P]).then_inc(k_hi_done, 1)

            def pair_q(pair):
                act.wait_ge(qk_hi_done, pair + 1)
                wait(act, s_acc, 2 * pair)
                source = full(qk_hi[0:R, pair & (PB - 1), :])
                rounded(qs_hi[0:R, :], source)
                rounded(qs_hi[R:2 * R, :], source).then_inc(qs_hi_done, 1)

            def exponentials(t, u):
                act.wait_ge(max_done, t + 1)
                nc.scalar.activation(probs[:], ps_s[:], ACT.Exp, bias=negmax[:, u:u + 1],
                                     accum_out=rowsum[:, u:u + 1]).then_inc(exp_done, 1)

            def probs_parts(t):
                for half in range(2):
                    act.wait_ge(pt_ps, 2 * t + half + 1)
                    rounded(pt_hi[:, HALF * half:HALF * (half + 1), :],
                            ps_t[half][:]).then_inc(pt_hi_done, 1)

            def normalize_x1(t, u):
                act.wait_ge(nmr2_done, t + 1)
                wait(act, h2_ps, t)
                nc.scalar.activation(x2n[:], x_ring[:, t & (2 * TB - 1), :], ACT.Identity,
                                     scale=rstd2[:, u:u + 1], bias=nmr2[:, u:u + 1]).then_inc(x2n_done, 1)

            def modulate_x1(t, b):
                act.wait_ge(h2_ps, t + 1)
                wait(act, h2_lo_done, t)
                modulate(h2_f, ps_t[0], b, 2).then_inc(h2_f_done, 1)

            def step(g, u, prep=True, next_x=True, next_norm=True, following=True, before=True, last_pair=False):
                t = 2 * g + u
                probs_parts(t)
                if prep:
                    values(t + TB)
                    if u:
                        qk(g + PB)
                if before:
                    modulate_x1(t - 1, batch_of(g - 1 + u))
                if next_x:
                    modulate_x(t + TB + 1, batch_of(g + u + PB))
                if following:
                    exponentials(t + 1, 1 - u)
                    if u == 0 and not last_pair:
                        pair_q(g + 1)
                if next_norm:
                    normalize_x(t + TB + 2, u)
                normalize_x1(t, u)

            act.wait_ge(c_loaded, 16)
            nc.scalar.activation(silu_den[:], c_sb[:], ACT.Exp, scale=-1.0).then_inc(silu_exp, 1)
            for m in range(C):
                act.wait_ge(wvo_acc, m + 1)
                rounded(wvo_hi[:, m, :], wvo_banks[m][:]).then_inc(wvo_hi_done, 1)
            act.wait_ge(wqk_loaded, 16)
            rounded(wqk_hi[:], wqk_raw[:]).then_inc(wqk_hi_done, 1)
            normalize_x(0, 0)
            act.wait_ge(mod_t_done, 2)
            modulate_x(0, 0)
            normalize_x(1, 1)

            def prep_pair(pair):
                for u in range(2):
                    q = 2 * pair + u
                    modulate_x(q + 1, batch_of(pair + u))
                    normalize_x(q + 2, u)
                    values(q)
                    if u:
                        qk(pair)

            prep_pair(0)
            with act.Fori(1, PB) as pair:
                prep_pair(pair)
            pair_q(0)
            exponentials(0, 0)
            act.wait_ge(mod_t_done, 4)
            act.wait_ge(f_added, 2 * (NF - 1))
            for k in range(C):
                rounded(f_hi[:, k, :], f_sum[:, k, :]).then_inc(f_hi_done, 1)
            step(0, 0, before=False)
            step(0, 1)
            with act.Fori(1, PAIRS - PB - 1) as g:
                for u in range(2):
                    step(g, u)
            step(PAIRS - PB - 1, 0, next_norm=False)
            step(PAIRS - PB - 1, 1, next_x=False, next_norm=False)
            with act.Fori(PAIRS - PB, PAIRS - 1) as g:
                for u in range(2):
                    step(g, u, prep=False, next_x=False, next_norm=False)
            step(PAIRS - 1, 0, prep=False, next_x=False, next_norm=False, last_pair=True)
            step(PAIRS - 1, 1, prep=False, next_x=False, next_norm=False, following=False)
            modulate_x1(T - 1, B - 1)

        @block.vector
        def _(dve):
            def rest(to, whole, hi):
                return nc.vector.tensor_tensor(to, whole, full(hi), ALU.subtract)

            def x_stats(q, u):
                nc.vector.bn_stats(stats1[:, u, :], x_ring[:, q & (2 * TB - 1), :]).then_inc(stats1_done, 1)
                wait_alone(dve, dve_passed, stats1_done, q + 1)
                nc.vector.bn_aggr(mv1[:, u, :], stats1[:, u, :]).then_inc(mv1_done, 1)

            def h_parts(q, pair, u):
                dve.wait_ge(h_f_done, q + 1)
                wait(dve, qk_acc, pair)
                here = slice(P * u, P * (u + 1))
                nc.vector.tensor_copy(h_hi[:, :, here], h_f[:]).then_inc(h_hi_done, 1)
                dve.wait_ge(h_hi_done, q + 1)
                rest(h_lo[:, :, here], h_f[:], h_hi[:, :, here]).then_inc(h_lo_done, 1)

            def values(q):
                dve.wait_ge(v_hi_done, q + 1)
                slot = q & (2 * TB - 1)
                rest(v_lo[:, slot, :], ps_v[:], v_hi[:, slot, :]).then_inc(v_lo_done, 1)

            def qk(pair):
                dve.wait_ge(qk_hi_done, pair + 1)
                slot = pair & (PB - 1)
                dve.wait_ge(k_hi_done, pair + 1)
                rest(qk_lo[:, slot, :], ps_qk[:, 0:2 * P], qk_hi[:, slot, :]).then_inc(qk_lo_done, 1)
                dve.wait_ge(qk_lo_done, pair + 1)
                nc.vector.tensor_copy(k_both[R:2 * R, pair & (2 * PB - 1), :],
                                      full(qk_lo[R:2 * R, slot, :])).then_inc(k_lo_done, 1)

            def pair_q(pair):
                dve.wait_ge(qk_lo_done, pair + 1)
                wait(dve, s_acc, 2 * pair)
                source = full(qk_lo[0:R, pair & (PB - 1), :])
                nc.vector.tensor_copy(qs_lo[0:R, :], source)
                nc.vector.tensor_copy(qs_lo[R:2 * R, :], source).then_inc(qs_lo_done, 1)

            def row_max(t, u):
                dve.wait_ge(s_acc, t + 1)
                nc.vector.tensor_reduce(negmax[:, u:u + 1], ps_s[:], AX_X, ALU.max,
                                        negate=True).then_inc(max_done, 1)

            def probs_rests(t):
                for half in range(2):
                    dve.wait_ge(pt_hi_done, 2 * t + half + 1)
                    here = slice(HALF * half, HALF * (half + 1))
                    rest(pt_lo[:, here, :], ps_t[half][:].rearrange("p (j i) -> p j i", i=P),
                         pt_hi[:, here, :]).then_inc(pt_lo_done, 1)

            def h2_parts(t):
                dve.wait_ge(h2_f_done, t + 1)
                nc.vector.tensor_copy(h2_hi[:], h2_f[:]).then_inc(h2_hi_done, 1)
                dve.wait_ge(h2_hi_done, t + 1)
                rest(h2_lo[:], h2_f[:], h2_hi[:]).then_inc(h2_lo_done, 1)

            def add_attention(t, u, b):
                dve.wait_ge(exp_done, t + 1)
                nc.vector.reciprocal(rden[:, u:u + 1], rowsum[:, u:u + 1]).then_inc(rden_done, 1)
                dve.wait_ge(o_acc, t + 1)
                dve.wait_ge(rden_done, t + 1)
                nc.vector.scalar_tensor_tensor(out=attn[:], in0=ps_o[:], scalar=rden[:, u:u + 1],
                                               in1=gates[:, 0, b, :], op0=ALU.mult,
                                               op1=ALU.mult).then_inc(attn_done, 1)
                dve.wait_ge(attn_done, t + 1)
                tile = x_ring[:, t & (2 * TB - 1), :]
                nc.vector.tensor_tensor(tile, attn[:], tile, ALU.add).then_inc(x1_done, 1)
                wait_alone(dve, dve_passed, x1_done, t + 1)
                nc.vector.bn_stats(stats2[:, u, :], tile).then_inc(stats2_done, 1)
                wait_alone(dve, dve_passed, stats2_done, t + 1)
                nc.vector.bn_aggr(mv2[:, u, :], stats2[:, u, :]).then_inc(mv2_done, 1)

            def ffn_out(t):
                dve.wait_ge(y_acc, t + 1)
                wait(dve, y_done, t)
                nc.vector.scalar_tensor_tensor(out=ffn[:], in0=ps_y[:], scalar=FSCALE, in1=bias_bc[:],
                                               op0=ALU.mult, op1=ALU.add).then_inc(ffn_done, 1)

            def step(g, u, prep=True, next_x=True, next_norm=True, following=True, before=True, last_pair=False):
                t = 2 * g + u
                probs_rests(t)
                if prep:
                    values(t + TB)
                    if u:
                        qk(g + PB)
                if following:
                    row_max(t + 1, 1 - u)
                    if u == 0 and not last_pair:
                        pair_q(g + 1)
                if before:
                    h2_parts(t - 1)
                if next_x:
                    h_parts(t + TB + 1, g + u + PB, 1 - u)
                if next_norm:
                    if u == 0:
                        wait_alone(dve, dve_passed, x_loaded, 16 * (g + PB + 2))
                    x_stats(t + TB + 2, u)
                add_attention(t, u, batch_of(g))
                if before:
                    ffn_out(t - 1)

            nc.vector.memset(minus_half[:], -0.5).then_inc(consts_set, 1)
            dve.wait_ge(silu_exp, 1)
            nc.vector.tensor_scalar(silu_den[:], silu_den[:], 1.0, None, ALU.add).then_inc(silu_steps, 1)
            dve.wait_ge(silu_steps, 1)
            nc.vector.reciprocal(silu_den[:], silu_den[:]).then_inc(silu_steps, 1)
            dve.wait_ge(silu_steps, 2)
            nc.vector.tensor_tensor(silu_c[:], c_sb[:], silu_den[:], ALU.mult).then_inc(silu_steps, 1)
            dve.wait_ge(x_loaded, 16)
            x_stats(0, 0)
            x_stats(1, 1)

            rows = [0]

            def row(v):
                nc.vector.tensor_copy(mod_rows[:, v, :], mod_banks[v][0:B, :]).then_inc(rows_done, 1)
                rows[0] += 1

            def gate_row(v):
                acc, sign, gate = mod_banks[v][0:B, :], mod_rows[:, GB + 1 + (v == GB), :], mod_rows[:, v, :]
                nc.vector.tensor_scalar(sign, acc, 0.0, 2.0, ALU.is_ge, ALU.mult).then_inc(rows_done, 1)
                dve.wait_ge(rows_done, rows[0] + 1)
                nc.vector.tensor_scalar(sign, sign, -1.0, None, ALU.add).then_inc(rows_done, 1)
                dve.wait_ge(rows_done, rows[0] + 2)
                nc.vector.tensor_tensor(gate, acc, sign, ALU.mult).then_inc(rows_done, 1)
                dve.wait_ge(rows_done, rows[0] + 3)
                nc.vector.scalar_tensor_tensor(out=gate, in0=gate, scalar=GATE_FLOOR, in1=sign,
                                               op0=ALU.max, op1=ALU.mult).then_inc(rows_done, 1)
                rows[0] += GATE_STEPS

            def columns(n):
                dve.wait_ge(mod_tps, n + 1)
                for i in range(2):
                    source = ps_t[0][:, i * C * B:(i + 1) * C * B].rearrange("p (c b) -> p b c", b=B)
                    nc.vector.tensor_scalar(mod_t[:, :, 2 * n + i, :], source, float(i), None,
                                            ALU.add).then_inc(mod_t_done, 1)

            for v in (SA, CA):
                dve.wait_ge(mod_acc, v + 1)
                row(v)
            columns(0)
            for m in range(C):
                dve.wait_ge(wvo_hi_done, m + 1)
                rest(wvo_lo[:, m, :], wvo_banks[m][:], wvo_hi[:, m, :]).then_inc(wvo_lo_done, 1)
            dve.wait_ge(wqk_hi_done, 1)
            rest(wqk_lo[:], wqk_raw[:], wqk_hi[:]).then_inc(wqk_lo_done, 1)
            for v in (GA, SB, CB, GB):
                dve.wait_ge(mod_acc, v + 1)
                if v in (GA, GB):
                    gate_row(v)
                else:
                    row(v)
            columns(1)
            h_parts(0, 0, 0)

            def prep_pair(pair):
                for u in range(2):
                    q = 2 * pair + u
                    h_parts(q + 1, pair + u, 1 - u)
                    if u == 0:
                        wait_alone(dve, dve_passed, x_loaded, 16 * (pair + 2))
                    x_stats(q + 2, u)
                    values(q)
                    if u:
                        qk(pair)

            prep_pair(0)
            with dve.Fori(1, PB) as pair:
                prep_pair(pair)
            pair_q(0)
            row_max(0, 0)
            for k in range(C):
                dve.wait_ge(f_hi_done, k + 1)
                rest(f_lo[:, k, :], f_sum[:, k, :], f_hi[:, k, :]).then_inc(f_lo_done, 1)
            dve.wait_ge(gates_loaded, 16)
            dve.wait_ge(bias_loaded, 16)
            step(0, 0, before=False)
            step(0, 1)
            with dve.Fori(1, PAIRS - PB - 1) as g:
                for u in range(2):
                    step(g, u)
            step(PAIRS - PB - 1, 0, next_norm=False)
            step(PAIRS - PB - 1, 1, next_x=False, next_norm=False)
            with dve.Fori(PAIRS - PB, PAIRS - 1) as g:
                for u in range(2):
                    step(g, u, prep=False, next_x=False, next_norm=False)
            last = PAIRS - 1
            step(last, 0, prep=False, next_x=False, next_norm=False, last_pair=True)
            step(last, 1, prep=False, next_x=False, next_norm=False, following=False)
            h2_parts(T - 1)
            ffn_out(T - 1)

        @block.gpsimd
        def _(pool):
            def inverse_std(count, u, mv, ve, rstd, nmr, mv_done, ve_done, rstd_done, nmr_done):
                wait_alone(pool, pool_passed, mv_done, count)
                one = slice(u, u + 1)
                nc.gpsimd.tensor_scalar(ve[:, one], mv[:, u, 1:2], EPS, None, ALU.add).then_inc(ve_done, 1)
                pool.wait_ge(ve_done, count)
                nc.gpsimd.tensor_tensor(rstd[:, one], ve[:, one], minus_half[:], ALU.pow).then_inc(rstd_done, 1)
                wait_alone(pool, pool_passed, rstd_done, count)
                nc.gpsimd.tensor_scalar(nmr[:, one], mv[:, u, 0:1], rstd[:, one], -1.0,
                                        ALU.mult, ALU.mult).then_inc(nmr_done, 1)

            def of_x(q, u):
                inverse_std(q + 1, u, mv1, ve1, rstd1, nmr1, mv1_done, ve1_done, rstd1_done, nmr1_done)

            def of_x1(t, u):
                inverse_std(t + 1, u, mv2, ve2, rstd2, nmr2, mv2_done, ve2_done, rstd2_done, nmr2_done)

            def result(t, b):
                pool.wait_ge(ffn_done, t + 1)
                nc.gpsimd.tensor_tensor(ffn[:], ffn[:], gates[:, 1, b, :], ALU.mult).then_inc(gated_done, 1)
                pool.wait_ge(gated_done, t + 1)
                tile = x_ring[:, t & (2 * TB - 1), :]
                nc.gpsimd.tensor_tensor(tile, ffn[:], tile, ALU.add).then_inc(y_done, 1)

            def step(g, u, next_norm=True, before=True):
                t = 2 * g + u
                if next_norm:
                    of_x(t + TB + 2, u)
                of_x1(t, u)
                if before:
                    result(t - 1, batch_of(g - 1 + u))

            nc.gpsimd.memset(ident[:], 0.0).then_inc(ident_set, 1)
            pool.wait_ge(ident_set, 1)
            nc.gpsimd.affine_select(out=ident[:], in_=ident[:], compare_op=ALU.not_equal, fill=1.0, base=0,
                                    pattern=[[-1, P]], channel_multiplier=1).then_inc(ident_set, 1)
            pool.wait_ge(consts_set, 1)
            of_x(0, 0)
            of_x(1, 1)
            pool.wait_ge(f0_loaded, 16)

            def add_factor(i):
                pool.wait_ge(stage_loaded[i % NS], 16 * (i // NS + 1))
                wait(pool, f_added, i - 1)
                half = f_sum[:, 2 * (i % 2):2 * (i % 2) + 2, :]
                nc.gpsimd.tensor_tensor(half, half, f_stage[:, i % NS], ALU.add).then_inc(f_added, 1)

            for q in range(2, TB + 2):
                if 2 * q - 3 < 2 * (NF - 1):
                    add_factor(2 * q - 4)
                    add_factor(2 * q - 3)
                of_x(q, q % 2)

            pool.wait_ge(rows_done, 4 + 2 * GATE_STEPS)
            pool.wait_ge(mod_tps, 2)
            pool.dma_start(gate_rows[0], mod_rows[:, GA, :]).then_inc(gates_stored, 16)
            pool.dma_start(gate_rows[1], mod_rows[:, GB, :]).then_inc(gates_stored, 16)
            pool.wait_ge(gates_stored, 32)
            pool.dma_start(gates[:].rearrange("p a b d -> p (a b d)"), gate_rows.rearrange(
                "a b d -> (a b d)").partition_broadcast(P)).then_inc(gates_loaded, 16)
            pool.wait_ge(gates_loaded, 16)
            step(0, 0, before=False)
            step(0, 1)
            with pool.Fori(1, PAIRS - PB - 1) as g:
                for u in range(2):
                    step(g, u)
            with pool.Fori(PAIRS - PB - 1, PAIRS) as g:
                for u in range(2):
                    step(g, u, next_norm=False)
            result(T - 1, B - 1)


_NAMES = ["x", "wqk_t", "wv", "wo_t", "factors", "bias", "c_t", "wmod"]


def kernel(L0_attn_hidden_states, L0_attn_Wq, L0_attn_Wk, L0_attn_Wv, L0_attn_Wo, L0_ffn_factors,
           L0_ffn_bias, L0_c, L0_wmod):
    import numpy as np
    import concourse.bacc as bacc
    from concourse.bass_utils import run_bass_kernel_spmd

    hidden = np.asarray(L0_attn_hidden_states)
    batch, seq, dim = hidden.shape
    c = np.asarray(L0_c)
    laid_out = [
        hidden.reshape(batch * seq, dim),
        np.concatenate([np.asarray(L0_attn_Wq), np.asarray(L0_attn_Wk)]).T,
        np.asarray(L0_attn_Wv),
        np.asarray(L0_attn_Wo).T,
        np.asarray(L0_ffn_factors),
        np.asarray(L0_ffn_bias),
        c.T.reshape(dim // P, P, batch).transpose(1, 0, 2).reshape(P, -1),
        np.asarray(L0_wmod),
    ]
    nc = bacc.Bacc("TRN2", target_bir_lowering=False, num_devices=1)
    arrays, args = {}, []
    for name, a in zip(_NAMES, laid_out):
        arrays[f"in_{name}"] = np.ascontiguousarray(a)
        args.append(nc.dram_tensor(f"in_{name}", a.shape, mybir.dt.from_np(a.dtype), kind="ExternalInput").ap())
    args.append(nc.dram_tensor("result", (batch * seq, dim), F32, kind="ExternalOutput").ap())
    adaln_block(nc, *args)
    r = run_bass_kernel_spmd(nc, [arrays], core_ids=[0])
    return r.results[0]["result"].reshape(batch, seq, dim)
```

```python
from contextlib import ExitStack

import concourse.bass as bass
from concourse import mybir

F32 = mybir.dt.float32
F32R = mybir.dt.float32r
ACT = mybir.ActivationFunctionType
ALU = mybir.AluOpType
AX_X = mybir.AxisListType.X

P = 128
EPS = 1e-5
GATE_STEPS = 4
GATE_FLOOR = 0.25
SA, CA, GA, SB, CB, GB = range(6)


def adaln_block(nc, x, wqk_t, wv, wo_t, factors, bias, c_t, wmod, out):
    tokens, D = x.shape
    B = c_t.shape[1] // (D // P)
    C = D // P
    TB = tokens // B // P
    T = tokens // P
    PAIRS, PB = T // 2, TB // 2
    KEYS = TB * P
    R = wqk_t.shape[1] // 2
    NF = factors.shape[0]
    HALF = TB // 2
    NS = 3
    FSCALE = 1.0 / float(NF) ** 0.5
    assert (P, D, R, C, TB, B) == (128, 512, 64, 4, 8, 4) and KEYS == 2 * D

    x_pairs = x.rearrange("(g u p) d -> g p u d", u=2, p=P)
    out_pairs = out.rearrange("(g u p) d -> g p u d", u=2, p=P)
    gate_rows = nc.dram_tensor("gate_rows", [2, B, D], F32, kind="Internal").ap()

    with ExitStack() as ctx:
        def sb(name, shape, dt=F32, stack=ctx):
            return stack.enter_context(nc.sbuf_tensor(name, shape, dt))

        def bank(name, columns=D):
            return ctx.enter_context(nc.psum_tensor(name, [P, columns], F32))

        def sem(name):
            return ctx.enter_context(nc.semaphore(name))

        ident = sb("ident", [P, P])
        c_sb = sb("c_sb", [P, C, B])
        silu_den = sb("silu_den", [P, C, B])
        silu_c = sb("silu_c", [P, C, B])
        mod_t = sb("mod_t", [P, B, 4, C])
        stats1 = sb("stats1", [P, 2, 6])
        stats2 = sb("stats2", [P, 2, 6])
        mv1 = sb("mv1", [P, 2, 2])
        mv2 = sb("mv2", [P, 2, 2])
        ve1 = sb("ve1", [P, 2])
        ve2 = sb("ve2", [P, 2])
        rstd1 = sb("rstd1", [P, 2])
        rstd2 = sb("rstd2", [P, 2])
        nmr1 = sb("nmr1", [P, 2])
        nmr2 = sb("nmr2", [P, 2])
        minus_half = sb("minus_half", [P, 1])
        negmax = sb("negmax", [P, 2])
        rowsum = sb("rowsum", [P, 2])
        rden = sb("rden", [P, 2])
        bias_bc = sb("bias_bc", [P, D])
        wvo_hi = sb("wvo_hi", [P, C, D], F32R)
        wvo_lo = sb("wvo_lo", [P, C, D], F32R)
        wqk_hi = sb("wqk_hi", [P, C, 2 * R], F32R)
        wqk_lo = sb("wqk_lo", [P, C, 2 * R], F32R)
        xn = sb("xn", [P, D])
        h_f = sb("h_f", [P, C, P])
        h_hi = sb("h_hi", [P, C, 2 * P], F32R)
        h_lo = sb("h_lo", [P, C, 2 * P], F32R)
        qk_hi = sb("qk_hi", [P, PB, 2 * P], F32R)
        qk_lo = sb("qk_lo", [P, PB, 2 * P], F32R)
        k_both = sb("k_both", [P, 2 * PB, 2 * P], F32R)
        gates = sb("gates", [P, 2, B, D])
        mod_rows = gates[0:B].rearrange("b a c d -> b (a c) d")

        with ExitStack() as setup:
            sb("under_x", [P, 2 * TB, D], F32, setup)
            sb("under_v_hi", [P, TB, D], F32, setup)
            wmod_0 = sb("wmod_0", [P, C, 2 * D], F32, setup)
            sb("under_v_lo", [P, TB, D], F32, setup)
            wmod_1 = sb("wmod_1", [P, C, 2 * D], F32, setup)
            wmod_2 = sb("wmod_2", [P, C, 2 * D], F32, setup)
            wqk_raw = sb("wqk_raw", [P, C, 2 * R], F32, setup)
            wv_raw = sb("wv_raw", [P, C, D], F32, setup)
            wo_raw = sb("wo_raw", [P, C, D], F32, setup)
        with ExitStack() as setup:
            sb("under_stage", [P, 3 * TB + 2, D], F32, setup)
            f_stage = sb("f_stage", [P, NS, 2, D], F32, setup)
            sb("under_sum", [P, TB + C, D], F32, setup)
            f_sum = sb("f_sum", [P, C, D], F32, setup)
        wmod_sb = [wmod_0, wmod_1, wmod_2]

        x_ring = sb("x_ring", [P, 2 * TB, D])
        v_hi = sb("v_hi", [P, 2 * TB, D], F32R)
        v_lo = sb("v_lo", [P, 2 * TB, D], F32R)
        pt_hi = sb("pt_hi", [P, TB, P], F32R)
        pt_lo = sb("pt_lo", [P, TB, P], F32R)
        h2_hi = sb("h2_hi", [P, C, P], F32R)
        h2_lo = sb("h2_lo", [P, C, P], F32R)
        x2n = sb("x2n", [P, D])
        attn = sb("attn", [P, D])
        ffn = sb("ffn", [P, D])
        f_hi = sb("f_hi", [P, C, D], F32R)
        f_lo = sb("f_lo", [P, C, D], F32R)
        probs = sb("probs", [P, KEYS])
        qs_hi = sb("qs_hi", [P, 2 * P], F32R)
        qs_lo = sb("qs_lo", [P, 2 * P], F32R)
        h2_f = sb("h2_f", [P, C, P])

        ps_s = bank("ps_s", KEYS)
        ps_t = [bank("ps_t0"), bank("ps_t1")]
        ps_v = bank("ps_v")
        ps_o = bank("ps_o")
        ps_y = bank("ps_y")
        ps_qk = bank("ps_qk")
        mod_banks = [ps_s[:, 0:D], ps_s[:, D:], ps_o[:], ps_y[:], ps_o[:], ps_y[:]]
        row_of = [0, 1, 2, 4, 5, 6]
        wvo_banks = [ps_v, ps_o, ps_y, ps_qk]

        c_loaded, wqk_loaded, bias_loaded, f0_loaded = (
            sem(n) for n in ("c_loaded", "wqk_loaded", "bias_loaded", "f0_loaded"))
        wmod_loaded = [[sem(f"wmod_loaded{i}_{k}") for k in range(C)] for i in range(3)]
        wv_loaded = [sem(f"wv_loaded{k}") for k in range(C)]
        wo_loaded = [sem(f"wo_loaded{k}") for k in range(C)]
        stage_loaded = [sem(f"stage_loaded{i}") for i in range(NS)]
        x_loaded = sem("x_loaded")
        y_stored = sem("y_stored")
        last_stored = sem("last_stored")
        gate_stored = [sem("ga_stored"), sem("gb_stored")]
        gate_loaded = [sem("ga_loaded"), sem("gb_loaded")]
        consts_set = sem("consts_set")
        ident_set = sem("ident_set")
        silu_exp, silu_steps = sem("silu_exp"), sem("silu_steps")
        mod_acc = sem("mod_acc")
        rows_done = sem("rows_done")
        mod_tps = sem("mod_tps")
        mod_t_done = sem("mod_t_done")
        wvo_acc, wvo_hi_done, wvo_lo_done = sem("wvo_acc"), sem("wvo_hi_done"), sem("wvo_lo_done")
        wqk_hi_done, wqk_lo_done = sem("wqk_hi_done"), sem("wqk_lo_done")
        f_added, f_hi_done, f_lo_done = sem("f_added"), sem("f_hi_done"), sem("f_lo_done")
        sp_passed, dve_passed, pool_passed = sem("sp_passed"), sem("dve_passed"), sem("pool_passed")
        stats1_done, mv1_done, ve1_done, rstd1_done, nmr1_done = (
            sem(n) for n in ("stats1_done", "mv1_done", "ve1_done", "rstd1_done", "nmr1_done"))
        xn_done, xt_ps, h_f_done, h_hi_done, h_lo_done = (
            sem(n) for n in ("xn_done", "xt_ps", "h_f_done", "h_hi_done", "h_lo_done"))
        v_acc, v_hi_done, v_lo_done = sem("v_acc"), sem("v_hi_done"), sem("v_lo_done")
        qk_acc, qk_hi_done, qk_lo_done, k_hi_done, k_lo_done = (
            sem(n) for n in ("qk_acc", "qk_hi_done", "qk_lo_done", "k_hi_done", "k_lo_done"))
        qs_hi_done, qs_lo_done = sem("qs_hi_done"), sem("qs_lo_done")
        s_acc, max_done, exp_done = sem("s_acc"), sem("max_done"), sem("exp_done")
        pt_ps, pt_hi_done, pt_lo_done, o_acc = (
            sem(n) for n in ("pt_ps", "pt_hi_done", "pt_lo_done", "o_acc"))
        rden_done, attn_done, x1_done = sem("rden_done"), sem("attn_done"), sem("x1_done")
        stats2_done, mv2_done, ve2_done, rstd2_done, nmr2_done = (
            sem(n) for n in ("stats2_done", "mv2_done", "ve2_done", "rstd2_done", "nmr2_done"))
        x2n_done, h2_ps, h2_f_done, h2_hi_done, h2_lo_done = (
            sem(n) for n in ("x2n_done", "h2_ps", "h2_f_done", "h2_hi_done", "h2_lo_done"))
        y_acc, ffn_done, gated_done, y_done = sem("y_acc"), sem("ffn_done"), sem("gated_done"), sem("y_done")

        def wait(eng, semaphore, value):
            if not isinstance(value, int) or value > 0:
                eng.wait_ge(semaphore, value)

        def wait_alone(eng, passed, semaphore, value):
            eng.wait_ge(semaphore, value)
            eng.sem_inc(passed, 1)

        def batch_of(pair):
            return (pair >> 2) & (B - 1)

        def full(ap):
            return ap.bitcast(F32)

        block = ctx.enter_context(nc.Block())

        @block.sync
        def _(sp):
            def load_x(pair):
                if not isinstance(pair, int) or pair > 0:
                    wait_alone(sp, sp_passed, x_loaded, pair * 16)
                slot = (pair & (2 * PB - 1)) * 2
                sp.dma_start(x_ring[:, bass.ds(slot, 2), :], x_pairs[pair]).then_inc(x_loaded, 16)

            def store_pair(pair):
                wait_alone(sp, sp_passed, y_done, 2 * pair + 2)
                if not isinstance(pair, int) or pair > 0:
                    wait_alone(sp, sp_passed, y_stored, pair * 16)
                slot = (pair & (2 * PB - 1)) * 2
                sp.dma_start(out_pairs[pair], x_ring[:, bass.ds(slot, 2), :]).then_inc(y_stored, 16)

            def load_rows(to, source, k, loaded):
                sp.dma_start(to[:, k, :], source[P * k:P * (k + 1), :]).then_inc(loaded[k], 16)

            def load_wmod(i):
                for k in range(C):
                    load_rows(wmod_sb[i], wmod[:, 2 * D * i:2 * D * (i + 1)], k, wmod_loaded[i])

            def spread_gate(i, vector):
                sp.dma_start(gate_rows[i], mod_rows[:, row_of[vector], :]).then_inc(gate_stored[i], 16)
                sp.wait_ge(gate_stored[i], 16)
                sp.dma_start(gates[:, i].rearrange("p b d -> p (b d)"), gate_rows[i].rearrange(
                    "b d -> (b d)").partition_broadcast(P)).then_inc(gate_loaded[i], 16)

            sp.dma_start(c_sb[:].rearrange("p c b -> p (c b)"), c_t).then_inc(c_loaded, 16)
            load_wmod(0)
            load_x(0)
            sp.dma_start(wqk_raw[:], wqk_t.rearrange("(c p) n -> p c n", p=P)).then_inc(wqk_loaded, 16)
            for k in range(C):
                load_rows(wv_raw, wv, k, wv_loaded)
                load_rows(wo_raw, wo_t, k, wo_loaded)
            load_x(1)
            load_wmod(1)
            load_x(2)
            load_x(3)
            load_wmod(2)
            sp.dma_start(bias_bc[:], bias.partition_broadcast(P)).then_inc(bias_loaded, 16)
            load_x(4)
            load_x(5)
            sp.wait_ge(mod_acc, SB + 1)
            sp.dma_start(f_sum[:], factors[0].rearrange("(c p) n -> p c n", p=P)).then_inc(f0_loaded, 16)
            for i in range(2 * (NF - 1)):
                if i == NS:
                    sp.wait_ge(rows_done, 2 + GATE_STEPS)
                    sp.wait_ge(mod_tps, 1)
                    spread_gate(0, GA)
                wait(sp, f_added, i - NS + 1)
                src = factors[1 + i // 2].rearrange("(h c p) n -> h p c n", h=2, p=P)[i % 2]
                sp.dma_start(f_stage[:, i % NS], src).then_inc(stage_loaded[i % NS], 16)
            load_x(6)
            load_x(7)
            sp.wait_ge(rows_done, 4 + 2 * GATE_STEPS)
            sp.wait_ge(mod_tps, 2)
            spread_gate(1, GB)

            def turn_over(pair):
                store_pair(pair)
                wait_alone(sp, sp_passed, y_stored, pair * 16 + 16)
                load_x(pair + 2 * PB)

            turn_over(0)
            with sp.Fori(1, PAIRS - 2 * PB) as pair:
                turn_over(pair)
            with sp.Fori(PAIRS - 2 * PB, PAIRS - 1) as pair:
                store_pair(pair)
            last = PAIRS - 1
            for u in range(2):
                sp.wait_ge(y_done, 2 * last + u + 1)
                sp.dma_start(out_pairs[last][:, u], x_ring[:, 2 * TB - 2 + u, :]).then_inc(last_stored, 16)
            sp.wait_ge(y_stored, last * 16)
            sp.wait_ge(last_stored, 32)

        @block.tensor
        def _(pe):
            def three(acc, a, b, first, last):
                (a_hi, a_lo), (b_hi, b_lo) = a, b
                nc.tensor.matmul(acc, a_hi, b_lo, start=first, stop=False)
                nc.tensor.matmul(acc, a_lo, b_hi, start=False, stop=False)
                return nc.tensor.matmul(acc, a_hi, b_hi, start=False, stop=last)

            def transposes(acc, source, n, base=0):
                for i in range(n):
                    last = nc.tensor.transpose(acc[:, P * i:P * (i + 1)],
                                               source[:, P * (base + i):P * (base + i + 1)], ident[:])
                return last

            def modulation(v):
                for k in range(C):
                    pe.wait_ge(wmod_loaded[v // 2][k], 16)
                    last = nc.tensor.matmul(mod_banks[v][0:B, :], silu_c[:, k, :],
                                            wmod_sb[v // 2][:, k, D * (v % 2):D * (v % 2 + 1)],
                                            start=(k == 0), stop=(k == C - 1))
                last.then_inc(mod_acc, 1)

            def modulation_columns(vectors):
                for i, v in enumerate(vectors):
                    for k in range(C):
                        at = (i * C + k) * B
                        last = nc.tensor.transpose(ps_t[0][:, at:at + B], mod_rows[:, row_of[v], P * k:P * (k + 1)],
                                                   ident[0:B, 0:B])
                last.then_inc(mod_tps, 1)

            def transpose_x(q):
                pe.wait_ge(xn_done, q + 1)
                wait(pe, h_f_done, q)
                transposes(ps_t[1], xn, C).then_inc(xt_ps, 1)

            def project_values(q, u):
                pe.wait_ge(h_lo_done, q + 1)
                wait(pe, v_lo_done, q)
                for k in range(C):
                    h = [part[:, k, P * u:P * (u + 1)] for part in (h_hi, h_lo)]
                    last = three(ps_v[:], h, (wvo_hi[:, k, :], wvo_lo[:, k, :]), k == 0, k == C - 1)
                last.then_inc(v_acc, 1)

            def project_qk(pair):
                wait(pe, qk_lo_done, pair)
                for k in range(C):
                    last = three(ps_qk[:, 0:2 * P], (wqk_hi[:, k, :], wqk_lo[:, k, :]),
                                 (h_hi[:, k, :], h_lo[:, k, :]), k == 0, k == C - 1)
                last.then_inc(qk_acc, 1)

            def scores(t, u, pair):
                pe.wait_ge(qs_hi_done, pair + 1)
                pe.wait_ge(qs_lo_done, pair + 1)
                pe.wait_ge(k_hi_done, (pair >> 2) * PB + PB)
                pe.wait_ge(k_lo_done, (pair >> 2) * PB + PB)
                wait(pe, exp_done, t)
                first = ((pair >> 2) & 1) * PB
                for n in range(2):
                    keys = k_both[:, bass.ds(first + 2 * n, 2), :]
                    acc = ps_s[:, D * n:D * (n + 1)]
                    nc.tensor.matmul(acc, qs_lo[:, P * u:P * (u + 1)], keys, start=True, stop=False)
                    last = nc.tensor.matmul(acc, qs_hi[:, P * u:P * (u + 1)], keys, start=False, stop=True)
                last.then_inc(s_acc, 1)

            def transpose_probs(t, prep):
                pe.wait_ge(exp_done, t + 1)
                wait(pe, h2_f_done, t - 1)
                transposes(ps_t[0], probs, HALF).then_inc(pt_ps, 1)
                if prep:
                    pe.wait_ge(h_f_done, t + TB + 1)
                wait(pe, pt_lo_done, 2 * t)
                transposes(ps_t[1], probs, HALF, HALF).then_inc(pt_ps, 1)

            def transpose_h2(t):
                pe.wait_ge(x2n_done, t + 1)
                pe.wait_ge(pt_lo_done, 2 * t + 3)
                transposes(ps_t[0], x2n, C).then_inc(h2_ps, 1)

            def attend(t, g, between=None):
                pe.wait_ge(v_lo_done, (g >> 2) * TB + TB)
                wait(pe, attn_done, t)
                first = ((g >> 2) & 1) * TB
                for j in range(TB):
                    if j % HALF == 0:
                        pe.wait_ge(pt_lo_done, 2 * t + 1 + j // HALF)
                    if j == HALF and between is not None:
                        transpose_h2(between)
                    v = [part[:, first + j, :] for part in (v_hi, v_lo)]
                    last = three(ps_o[:], (pt_hi[:, j, :], pt_lo[:, j, :]), v, j == 0, j == TB - 1)
                last.then_inc(o_acc, 1)

            def feed_forward(t):
                pe.wait_ge(h2_lo_done, t + 1)
                wait(pe, ffn_done, t)
                for k in range(C):
                    last = three(ps_y[:], (h2_hi[:, k, :], h2_lo[:, k, :]),
                                 (f_hi[:, k, :], f_lo[:, k, :]), k == 0, k == C - 1)
                last.then_inc(y_acc, 1)

            def prep_pair(pair):
                for u in range(2):
                    if u:
                        pe.wait_ge(h_lo_done, 2 * pair + 2)
                        project_qk(pair)
                    transpose_x(2 * pair + u + 1)
                    project_values(2 * pair + u, u)

            def step(g, u, prep=True, next_x=True, following=True, older=2):
                t = 2 * g + u
                transpose_probs(t, prep)
                if older == 2:
                    feed_forward(t - 2)
                if prep:
                    if u:
                        pe.wait_ge(h_lo_done, t + TB + 1)
                        project_qk(g + PB)
                    project_values(t + TB, u)
                if following:
                    scores(t + 1, 1 - u, g + u)
                if next_x:
                    pe.wait_ge(pt_lo_done, 2 * t + 2)
                    transpose_x(t + TB + 1)
                attend(t, g, t - 1 if older else None)

            pe.wait_ge(silu_steps, 3)
            modulation(SA)
            modulation(CA)
            pe.wait_ge(ident_set, 2)
            transpose_x(0)
            pe.wait_ge(rows_done, 2)
            modulation_columns((SA, CA))
            for k in range(C):
                pe.wait_ge(wv_loaded[k], 16)
                pe.wait_ge(wo_loaded[k], 16)
                for m in range(C):
                    last = nc.tensor.matmul(wvo_banks[m][:], wv_raw[:, k, P * m:P * (m + 1)], wo_raw[:, k, :],
                                            start=(k == 0), stop=(k == C - 1))
                    if k == C - 1:
                        last.then_inc(wvo_acc, 1)
            pe.wait_ge(wqk_lo_done, 1)
            pe.wait_ge(wvo_lo_done, C)
            prep_pair(0)
            modulation(GA)
            modulation(SB)
            with pe.Fori(1, PB) as pair:
                prep_pair(pair)
            scores(0, 0, 0)
            pe.wait_ge(rows_done, 3 + GATE_STEPS)
            modulation(CB)
            modulation(GB)
            pe.wait_ge(mod_t_done, 2)
            pe.wait_ge(rows_done, 4 + GATE_STEPS)
            modulation_columns((SB, CB))
            pe.wait_ge(mod_t_done, 4)
            pe.wait_ge(rows_done, 4 + 2 * GATE_STEPS)
            step(0, 0, older=0)
            step(0, 1, older=1)
            pe.wait_ge(f_hi_done, C)
            pe.wait_ge(f_lo_done, C)
            with pe.Fori(1, PAIRS - PB - 1) as g:
                for u in range(2):
                    step(g, u)
            step(PAIRS - PB - 1, 0)
            step(PAIRS - PB - 1, 1, next_x=False)
            with pe.Fori(PAIRS - PB, PAIRS - 1) as g:
                for u in range(2):
                    step(g, u, prep=False, next_x=False)
            step(PAIRS - 1, 0, prep=False, next_x=False)
            step(PAIRS - 1, 1, prep=False, next_x=False, following=False)
            feed_forward(T - 2)
            pe.wait_ge(x2n_done, T)
            transposes(ps_t[0], x2n, C).then_inc(h2_ps, 1)
            feed_forward(T - 1)

        @block.scalar
        def _(act):
            def rounded(to, source):
                return nc.scalar.activation(to, source, ACT.Identity)

            def modulate(to, source, b, v):
                for k in range(C):
                    last = nc.scalar.activation(to[:, k, :], source[:, P * k:P * (k + 1)], ACT.Identity,
                                                scale=mod_t[:, b, v + 1, k:k + 1], bias=mod_t[:, b, v, k:k + 1])
                return last

            def normalize_x(q, u):
                act.wait_ge(nmr1_done, q + 1)
                wait(act, xt_ps, q)
                nc.scalar.activation(xn[:], x_ring[:, q & (2 * TB - 1), :], ACT.Identity,
                                     scale=rstd1[:, u:u + 1], bias=nmr1[:, u:u + 1]).then_inc(xn_done, 1)

            def modulate_x(q, b):
                act.wait_ge(xt_ps, q + 1)
                wait(act, h_lo_done, q)
                modulate(h_f, ps_t[1], b, 0).then_inc(h_f_done, 1)

            def values(q):
                act.wait_ge(v_acc, q + 1)
                rounded(v_hi[:, q & (2 * TB - 1), :], ps_v[:]).then_inc(v_hi_done, 1)

            def qk(pair):
                act.wait_ge(qk_acc, pair + 1)
                rounded(qk_hi[:, pair & (PB - 1), :], ps_qk[:, 0:2 * P]).then_inc(qk_hi_done, 1)
                rounded(k_both[0:R, pair & (2 * PB - 1), :], ps_qk[R:2 * R, 0:2 * P]).then_inc(k_hi_done, 1)

            def pair_q(pair):
                act.wait_ge(qk_hi_done, pair + 1)
                wait(act, s_acc, 2 * pair)
                source = full(qk_hi[0:R, pair & (PB - 1), :])
                rounded(qs_hi[0:R, :], source)
                rounded(qs_hi[R:2 * R, :], source).then_inc(qs_hi_done, 1)

            def exponentials(t, u):
                act.wait_ge(max_done, t + 1)
                nc.scalar.activation(probs[:], ps_s[:], ACT.Exp, bias=negmax[:, u:u + 1],
                                     accum_out=rowsum[:, u:u + 1]).then_inc(exp_done, 1)

            def probs_parts(t):
                for half in range(2):
                    act.wait_ge(pt_ps, 2 * t + half + 1)
                    rounded(pt_hi[:, HALF * half:HALF * (half + 1), :],
                            ps_t[half][:]).then_inc(pt_hi_done, 1)

            def normalize_x1(t, u):
                act.wait_ge(nmr2_done, t + 1)
                wait(act, h2_ps, t)
                nc.scalar.activation(x2n[:], x_ring[:, t & (2 * TB - 1), :], ACT.Identity,
                                     scale=rstd2[:, u:u + 1], bias=nmr2[:, u:u + 1]).then_inc(x2n_done, 1)

            def modulate_x1(t, b):
                act.wait_ge(h2_ps, t + 1)
                wait(act, h2_lo_done, t)
                modulate(h2_f, ps_t[0], b, 2).then_inc(h2_f_done, 1)

            def step(g, u, prep=True, next_x=True, next_norm=True, following=True, older=2, last_pair=False):
                t = 2 * g + u
                probs_parts(t)
                if prep and u:
                    qk(g + PB)
                if older:
                    normalize_x1(t - 1, 1 - u)
                if prep:
                    values(t + TB)
                if next_x:
                    modulate_x(t + TB + 1, batch_of(g + u + PB))
                if following:
                    exponentials(t + 1, 1 - u)
                    if u == 0 and not last_pair:
                        pair_q(g + 1)
                if older:
                    modulate_x1(t - 1, batch_of(g - 1 + u))
                if next_norm:
                    normalize_x(t + TB + 2, u)

            def prep_pair(pair):
                for u in range(2):
                    q = 2 * pair + u
                    if u:
                        qk(pair)
                    modulate_x(q + 1, batch_of(pair + u))
                    normalize_x(q + 2, u)
                    values(q)

            act.wait_ge(c_loaded, 16)
            nc.scalar.activation(silu_den[:], c_sb[:], ACT.Exp, scale=-1.0).then_inc(silu_exp, 1)
            normalize_x(0, 0)
            act.wait_ge(wqk_loaded, 16)
            rounded(wqk_hi[:], wqk_raw[:]).then_inc(wqk_hi_done, 1)
            act.wait_ge(mod_t_done, 2)
            modulate_x(0, 0)
            normalize_x(1, 1)
            for m in range(C):
                act.wait_ge(wvo_acc, m + 1)
                rounded(wvo_hi[:, m, :], wvo_banks[m][:]).then_inc(wvo_hi_done, 1)
            prep_pair(0)
            with act.Fori(1, PB) as pair:
                prep_pair(pair)
            pair_q(0)
            exponentials(0, 0)
            step(0, 0, older=0)
            act.wait_ge(f_added, 2 * (NF - 1))
            for k in range(C):
                rounded(f_hi[:, k, :], f_sum[:, k, :]).then_inc(f_hi_done, 1)
            act.wait_ge(mod_t_done, 4)
            step(0, 1, older=1)
            with act.Fori(1, PAIRS - PB - 1) as g:
                for u in range(2):
                    step(g, u)
            step(PAIRS - PB - 1, 0, next_norm=False)
            step(PAIRS - PB - 1, 1, next_x=False, next_norm=False)
            with act.Fori(PAIRS - PB, PAIRS - 1) as g:
                for u in range(2):
                    step(g, u, prep=False, next_x=False, next_norm=False)
            step(PAIRS - 1, 0, prep=False, next_x=False, next_norm=False, last_pair=True)
            step(PAIRS - 1, 1, prep=False, next_x=False, next_norm=False, following=False)
            normalize_x1(T - 1, 1)
            modulate_x1(T - 1, B - 1)

        @block.vector
        def _(dve):
            def rest(to, whole, hi):
                return nc.vector.tensor_tensor(to, whole, full(hi), ALU.subtract)

            def x_stats(q, u):
                nc.vector.bn_stats(stats1[:, u, :], x_ring[:, q & (2 * TB - 1), :]).then_inc(stats1_done, 1)
                wait_alone(dve, dve_passed, stats1_done, q + 1)
                nc.vector.bn_aggr(mv1[:, u, :], stats1[:, u, :]).then_inc(mv1_done, 1)

            def h_parts(q, pair, u):
                dve.wait_ge(h_f_done, q + 1)
                wait(dve, qk_acc, pair)
                here = slice(P * u, P * (u + 1))
                nc.vector.tensor_copy(h_hi[:, :, here], h_f[:]).then_inc(h_hi_done, 1)
                dve.wait_ge(h_hi_done, q + 1)
                rest(h_lo[:, :, here], h_f[:], h_hi[:, :, here]).then_inc(h_lo_done, 1)

            def values(q):
                dve.wait_ge(v_hi_done, q + 1)
                slot = q & (2 * TB - 1)
                rest(v_lo[:, slot, :], ps_v[:], v_hi[:, slot, :]).then_inc(v_lo_done, 1)

            def qk(pair):
                dve.wait_ge(qk_hi_done, pair + 1)
                slot = pair & (PB - 1)
                dve.wait_ge(k_hi_done, pair + 1)
                rest(qk_lo[:, slot, :], ps_qk[:, 0:2 * P], qk_hi[:, slot, :]).then_inc(qk_lo_done, 1)
                dve.wait_ge(qk_lo_done, pair + 1)
                nc.vector.tensor_copy(k_both[R:2 * R, pair & (2 * PB - 1), :],
                                      full(qk_lo[R:2 * R, slot, :])).then_inc(k_lo_done, 1)

            def pair_q(pair):
                dve.wait_ge(qk_lo_done, pair + 1)
                wait(dve, s_acc, 2 * pair)
                source = full(qk_lo[0:R, pair & (PB - 1), :])
                nc.vector.tensor_copy(qs_lo[0:R, :], source)
                nc.vector.tensor_copy(qs_lo[R:2 * R, :], source).then_inc(qs_lo_done, 1)

            def row_max(t, u):
                dve.wait_ge(s_acc, t + 1)
                nc.vector.tensor_reduce(negmax[:, u:u + 1], ps_s[:], AX_X, ALU.max,
                                        negate=True).then_inc(max_done, 1)

            def probs_rest(t, half):
                dve.wait_ge(pt_hi_done, 2 * t + half + 1)
                here = slice(HALF * half, HALF * (half + 1))
                rest(pt_lo[:, here, :], ps_t[half][:].rearrange("p (j i) -> p j i", i=P),
                     pt_hi[:, here, :]).then_inc(pt_lo_done, 1)

            def h2_parts(t):
                dve.wait_ge(h2_f_done, t + 1)
                nc.vector.tensor_copy(h2_hi[:], h2_f[:]).then_inc(h2_hi_done, 1)
                dve.wait_ge(h2_hi_done, t + 1)
                rest(h2_lo[:], h2_f[:], h2_hi[:]).then_inc(h2_lo_done, 1)

            def add_attention(t, u, b):
                dve.wait_ge(exp_done, t + 1)
                nc.vector.reciprocal(rden[:, u:u + 1], rowsum[:, u:u + 1]).then_inc(rden_done, 1)
                dve.wait_ge(o_acc, t + 1)
                dve.wait_ge(rden_done, t + 1)
                nc.vector.scalar_tensor_tensor(out=attn[:], in0=ps_o[:], scalar=rden[:, u:u + 1],
                                               in1=gates[:, 0, b, :], op0=ALU.mult,
                                               op1=ALU.mult).then_inc(attn_done, 1)
                dve.wait_ge(attn_done, t + 1)
                tile = x_ring[:, t & (2 * TB - 1), :]
                nc.vector.tensor_tensor(tile, attn[:], tile, ALU.add).then_inc(x1_done, 1)

            def x1_stats(t, u):
                tile = x_ring[:, t & (2 * TB - 1), :]
                wait_alone(dve, dve_passed, x1_done, t + 1)
                nc.vector.bn_stats(stats2[:, u, :], tile).then_inc(stats2_done, 1)
                wait_alone(dve, dve_passed, stats2_done, t + 1)
                nc.vector.bn_aggr(mv2[:, u, :], stats2[:, u, :]).then_inc(mv2_done, 1)

            def ffn_out(t):
                dve.wait_ge(y_acc, t + 1)
                wait(dve, y_done, t)
                nc.vector.scalar_tensor_tensor(out=ffn[:], in0=ps_y[:], scalar=FSCALE, in1=bias_bc[:],
                                               op0=ALU.mult, op1=ALU.add).then_inc(ffn_done, 1)

            def step(g, u, prep=True, next_x=True, next_norm=True, following=True, older=2, last_pair=False):
                t = 2 * g + u
                probs_rest(t, 0)
                if older:
                    x1_stats(t - 1, 1 - u)
                probs_rest(t, 1)
                if older == 2:
                    ffn_out(t - 2)
                if prep:
                    if u:
                        qk(g + PB)
                    values(t + TB)
                if following:
                    row_max(t + 1, 1 - u)
                    if u == 0 and not last_pair:
                        pair_q(g + 1)
                if next_norm:
                    if u == 0:
                        wait_alone(dve, dve_passed, x_loaded, 16 * (g + PB + 2))
                    x_stats(t + TB + 2, u)
                if next_x:
                    h_parts(t + TB + 1, g + u + PB, 1 - u)
                if older:
                    h2_parts(t - 1)
                add_attention(t, u, batch_of(g))

            def prep_pair(pair):
                for u in range(2):
                    q = 2 * pair + u
                    if u:
                        qk(pair)
                    if u == 0:
                        wait_alone(dve, dve_passed, x_loaded, 16 * (pair + 2))
                    x_stats(q + 2, u)
                    h_parts(q + 1, pair + u, 1 - u)
                    values(q)

            nc.vector.memset(minus_half[:], -0.5).then_inc(consts_set, 1)
            dve.wait_ge(silu_exp, 1)
            nc.vector.tensor_scalar(silu_den[:], silu_den[:], 1.0, None, ALU.add).then_inc(silu_steps, 1)
            dve.wait_ge(silu_steps, 1)
            nc.vector.reciprocal(silu_den[:], silu_den[:]).then_inc(silu_steps, 1)
            dve.wait_ge(silu_steps, 2)
            nc.vector.tensor_tensor(silu_c[:], c_sb[:], silu_den[:], ALU.mult).then_inc(silu_steps, 1)
            dve.wait_ge(x_loaded, 16)
            x_stats(0, 0)
            x_stats(1, 1)

            rows = [0]

            def row(v):
                dve.wait_ge(mod_acc, v + 1)
                nc.vector.tensor_copy(mod_rows[:, row_of[v], :], mod_banks[v][0:B, :]).then_inc(rows_done, 1)
                rows[0] += 1

            def gate_row(v):
                dve.wait_ge(mod_acc, v + 1)
                acc, gate, sign = mod_banks[v][0:B, :], mod_rows[:, row_of[v], :], mod_rows[:, row_of[v] + 1, :]
                nc.vector.tensor_scalar(sign, acc, 0.0, 2.0, ALU.is_ge, ALU.mult).then_inc(rows_done, 1)
                dve.wait_ge(rows_done, rows[0] + 1)
                nc.vector.tensor_scalar(sign, sign, -1.0, None, ALU.add).then_inc(rows_done, 1)
                dve.wait_ge(rows_done, rows[0] + 2)
                nc.vector.tensor_tensor(gate, acc, sign, ALU.mult).then_inc(rows_done, 1)
                dve.wait_ge(rows_done, rows[0] + 3)
                nc.vector.scalar_tensor_tensor(out=gate, in0=gate, scalar=GATE_FLOOR, in1=sign,
                                               op0=ALU.max, op1=ALU.mult).then_inc(rows_done, 1)
                rows[0] += GATE_STEPS

            def columns(n):
                dve.wait_ge(mod_tps, n + 1)
                for i in range(2):
                    source = ps_t[0][:, i * C * B:(i + 1) * C * B].rearrange("p (c b) -> p b c", b=B)
                    nc.vector.tensor_scalar(mod_t[:, :, 2 * n + i, :], source, float(i), None,
                                            ALU.add).then_inc(mod_t_done, 1)

            row(SA)
            row(CA)
            columns(0)
            dve.wait_ge(wqk_hi_done, 1)
            rest(wqk_lo[:], wqk_raw[:], wqk_hi[:]).then_inc(wqk_lo_done, 1)
            h_parts(0, 0, 0)
            for m in range(C):
                dve.wait_ge(wvo_hi_done, m + 1)
                rest(wvo_lo[:, m, :], wvo_banks[m][:], wvo_hi[:, m, :]).then_inc(wvo_lo_done, 1)
            prep_pair(0)
            gate_row(GA)
            row(SB)
            with dve.Fori(1, PB) as pair:
                prep_pair(pair)
            pair_q(0)
            row_max(0, 0)
            row(CB)
            columns(1)
            gate_row(GB)
            dve.wait_ge(gate_loaded[0], 16)
            dve.wait_ge(bias_loaded, 16)
            step(0, 0, older=0)
            for k in range(C):
                dve.wait_ge(f_hi_done, k + 1)
                rest(f_lo[:, k, :], f_sum[:, k, :], f_hi[:, k, :]).then_inc(f_lo_done, 1)
            step(0, 1, older=1)
            with dve.Fori(1, PAIRS - PB - 1) as g:
                for u in range(2):
                    step(g, u)
            step(PAIRS - PB - 1, 0, next_norm=False)
            step(PAIRS - PB - 1, 1, next_x=False, next_norm=False)
            with dve.Fori(PAIRS - PB, PAIRS - 1) as g:
                for u in range(2):
                    step(g, u, prep=False, next_x=False, next_norm=False)
            step(PAIRS - 1, 0, prep=False, next_x=False, next_norm=False, last_pair=True)
            step(PAIRS - 1, 1, prep=False, next_x=False, next_norm=False, following=False)
            x1_stats(T - 1, 1)
            ffn_out(T - 2)
            h2_parts(T - 1)
            ffn_out(T - 1)

        @block.gpsimd
        def _(pool):
            def inverse_std(count, u, mv, ve, rstd, nmr, mv_done, ve_done, rstd_done, nmr_done):
                wait_alone(pool, pool_passed, mv_done, count)
                one = slice(u, u + 1)
                nc.gpsimd.tensor_scalar(ve[:, one], mv[:, u, 1:2], EPS, None, ALU.add).then_inc(ve_done, 1)
                pool.wait_ge(ve_done, count)
                nc.gpsimd.tensor_tensor(rstd[:, one], ve[:, one], minus_half[:], ALU.pow).then_inc(rstd_done, 1)
                wait_alone(pool, pool_passed, rstd_done, count)
                nc.gpsimd.tensor_scalar(nmr[:, one], mv[:, u, 0:1], rstd[:, one], -1.0,
                                        ALU.mult, ALU.mult).then_inc(nmr_done, 1)

            def of_x(q, u):
                inverse_std(q + 1, u, mv1, ve1, rstd1, nmr1, mv1_done, ve1_done, rstd1_done, nmr1_done)

            def of_x1(t, u):
                inverse_std(t + 1, u, mv2, ve2, rstd2, nmr2, mv2_done, ve2_done, rstd2_done, nmr2_done)

            def result(t, b):
                wait_alone(pool, pool_passed, ffn_done, t + 1)
                nc.gpsimd.tensor_tensor(ffn[:], ffn[:], gates[:, 1, b, :], ALU.mult).then_inc(gated_done, 1)
                wait_alone(pool, pool_passed, gated_done, t + 1)
                tile = x_ring[:, t & (2 * TB - 1), :]
                nc.gpsimd.tensor_tensor(tile, ffn[:], tile, ALU.add).then_inc(y_done, 1)

            def step(g, u, next_norm=True, older=2):
                t = 2 * g + u
                if older == 2:
                    result(t - 2, batch_of(g - 1))
                if next_norm:
                    of_x(t + TB + 2, u)
                of_x1(t, u)

            nc.gpsimd.memset(ident[:], 0.0).then_inc(ident_set, 1)
            pool.wait_ge(ident_set, 1)
            nc.gpsimd.affine_select(out=ident[:], in_=ident[:], compare_op=ALU.not_equal, fill=1.0, base=0,
                                    pattern=[[-1, P]], channel_multiplier=1).then_inc(ident_set, 1)
            pool.wait_ge(consts_set, 1)
            of_x(0, 0)
            of_x(1, 1)

            def add_factor(i):
                pool.wait_ge(f0_loaded, 16)
                pool.wait_ge(stage_loaded[i % NS], 16 * (i // NS + 1))
                wait(pool, f_added, i - 1)
                half = f_sum[:, 2 * (i % 2):2 * (i % 2) + 2, :]
                nc.gpsimd.tensor_tensor(half, half, f_stage[:, i % NS], ALU.add).then_inc(f_added, 1)

            added = 0
            for q in range(2, TB + 2):
                of_x(q, q % 2)
                for _ in range((0, 0, 2, 2, 2, 2, 3, 3)[q - 2]):
                    add_factor(added)
                    added += 1
            step(0, 0, older=0)
            step(0, 1, older=1)
            pool.wait_ge(gate_loaded[1], 16)
            with pool.Fori(1, PAIRS - PB - 1) as g:
                for u in range(2):
                    step(g, u)
            with pool.Fori(PAIRS - PB - 1, PAIRS) as g:
                for u in range(2):
                    step(g, u, next_norm=False)
            result(T - 2, B - 1)
            result(T - 1, B - 1)


_NAMES = ["x", "wqk_t", "wv", "wo_t", "factors", "bias", "c_t", "wmod"]


def kernel(L0_attn_hidden_states, L0_attn_Wq, L0_attn_Wk, L0_attn_Wv, L0_attn_Wo, L0_ffn_factors,
           L0_ffn_bias, L0_c, L0_wmod):
    import numpy as np
    import concourse.bacc as bacc
    from concourse.bass_utils import run_bass_kernel_spmd

    hidden = np.asarray(L0_attn_hidden_states)
    batch, seq, dim = hidden.shape
    c = np.asarray(L0_c)
    laid_out = [
        hidden.reshape(batch * seq, dim),
        np.concatenate([np.asarray(L0_attn_Wq), np.asarray(L0_attn_Wk)]).T,
        np.asarray(L0_attn_Wv),
        np.asarray(L0_attn_Wo).T,
        np.asarray(L0_ffn_factors),
        np.asarray(L0_ffn_bias),
        c.T.reshape(dim // P, P, batch).transpose(1, 0, 2).reshape(P, -1),
        np.asarray(L0_wmod),
    ]
    nc = bacc.Bacc("TRN2", target_bir_lowering=False, num_devices=1)
    arrays, args = {}, []
    for name, a in zip(_NAMES, laid_out):
        arrays[f"in_{name}"] = np.ascontiguousarray(a)
        args.append(nc.dram_tensor(f"in_{name}", a.shape, mybir.dt.from_np(a.dtype), kind="ExternalInput").ap())
    args.append(nc.dram_tensor("result", (batch * seq, dim), F32, kind="ExternalOutput").ap())
    adaln_block(nc, *args)
    r = run_bass_kernel_spmd(nc, [arrays], core_ids=[0])
    return r.results[0]["result"].reshape(batch, seq, dim)
```

```python
from contextlib import ExitStack

import concourse.bass as bass
from concourse import mybir

F32 = mybir.dt.float32
F32R = mybir.dt.float32r
ACT = mybir.ActivationFunctionType
ALU = mybir.AluOpType
AX_X = mybir.AxisListType.X

P = 128
EPS = 1e-5
GATE_FLOOR = 0.25
SA, CA, GA, SB, CB, GB = range(6)
WARMUPS = 7
LO_ROW = 32
ROWS_DONE = [1, 2, 8, 10, 12, 18]


def adaln_block(nc, x, wqk_t, wv, wo_t, factors, bias, c_t, wmod, out):
    tokens, D = x.shape
    B = c_t.shape[1] // (D // P)
    C = D // P
    TB = tokens // B // P
    T = tokens // P
    PAIRS, PB = T // 2, TB // 2
    KEYS = TB * P
    R = wqk_t.shape[1] // 2
    NF = factors.shape[0]
    HALF = TB // 2
    FSCALE = 1.0 / float(NF) ** 0.5
    assert (P, D, R, C, TB, B) == (128, 512, 64, 4, 8, 4) and KEYS == 2 * D

    x_pairs = x.rearrange("(g u p) d -> g p u d", u=2, p=P)
    out_pairs = out.rearrange("(g u p) d -> g p u d", u=2, p=P)
    gate_rows = nc.dram_tensor("gate_rows", [2, B, D], F32, kind="Internal").ap()

    with ExitStack() as ctx:
        def sb(name, shape, dt=F32, stack=ctx):
            return stack.enter_context(nc.sbuf_tensor(name, shape, dt))

        def bank(name, columns=D):
            return ctx.enter_context(nc.psum_tensor(name, [P, columns], F32))

        def sem(name):
            return ctx.enter_context(nc.semaphore(name))

        ident = sb("ident", [P, P])
        c_sb = sb("c_sb", [P, C, B])
        silu_den = sb("silu_den", [P, C, B])
        silu_c = sb("silu_c", [P, C, B])
        silu_parts = sb("silu_parts", [P, C, LO_ROW + B], F32R)
        no_parts = sb("no_parts", [P, C, LO_ROW + B])
        mod_t = sb("mod_t", [P, B, 4, C])
        stats1 = sb("stats1", [P, 2, 6])
        stats2 = sb("stats2", [P, 2, 6])
        mv1 = sb("mv1", [P, 2, 2])
        mv2 = sb("mv2", [P, 2, 2])
        ve1 = sb("ve1", [P, 2])
        ve2 = sb("ve2", [P, 2])
        rstd1 = sb("rstd1", [P, 2])
        rstd2 = sb("rstd2", [P, 2])
        nmr1 = sb("nmr1", [P, 2])
        nmr2 = sb("nmr2", [P, 2])
        minus_half = sb("minus_half", [P, 1])
        negmax = sb("negmax", [P, 2])
        rowsum = sb("rowsum", [P, 2])
        rden = sb("rden", [P, 2])
        bias_bc = sb("bias_bc", [P, D])
        wvo_hi = sb("wvo_hi", [P, C, D], F32R)
        wvo_lo = sb("wvo_lo", [P, C, D], F32R)
        wqk_hi = sb("wqk_hi", [P, C, 2 * R], F32R)
        wqk_lo = sb("wqk_lo", [P, C, 2 * R], F32R)
        xn = sb("xn", [P, D])
        h_f = sb("h_f", [P, C, P])
        h_hi = sb("h_hi", [P, C, 2 * P], F32R)
        h_lo = sb("h_lo", [P, C, 2 * P], F32R)
        qk_hi = sb("qk_hi", [P, PB, 2 * P], F32R)
        qk_lo = sb("qk_lo", [P, PB, 2 * P], F32R)
        k_both = sb("k_both", [P, 2 * PB, 2 * P], F32R)
        gates = sb("gates", [P, 2, B, D])
        mod_rows = gates[0:B].rearrange("b a c d -> b (a c) d")

        with ExitStack() as setup:
            sb("under_x", [P, 2 * TB, D], F32, setup)
            sb("under_v_hi", [P, TB, D], F32, setup)
            wmod_0 = sb("wmod_0", [P, C, 2 * D], F32, setup)
            sb("under_v_lo", [P, TB, D], F32, setup)
            wmod_1 = sb("wmod_1", [P, C, 2 * D], F32, setup)
            wmod_2 = sb("wmod_2", [P, C, 2 * D], F32, setup)
            wqk_raw = sb("wqk_raw", [P, C, 2 * R], F32, setup)
            wv_raw = sb("wv_raw", [P, C, D], F32, setup)
            wo_raw = sb("wo_raw", [P, C, D], F32, setup)
        with ExitStack() as setup:
            sb("under_parts", [P, TB, D], F32, setup)
            w_parts = [sb("w_part_0", [P, C, D], F32R, setup), sb("w_part_1", [P, C, D], F32R, setup)]
            sb("under_more", [P, TB, D], F32, setup)
            w_parts += [sb("w_part_2", [P, C, D], F32R, setup), sb("w_part_3", [P, C, D], F32R, setup)]
            sb("under_last", [P, TB, D], F32, setup)
            w_parts += [sb("w_part_4", [P, C, D], F32R, setup)]
            f_sum = sb("f_sum", [P, C, D], F32, setup)
        wmod_sb = [wmod_0, wmod_1, wmod_2]
        w_hi = {GA: w_parts[0], SB: w_parts[1], CB: w_parts[4], GB: w_parts[1]}
        w_lo = {GA: w_parts[2], SB: w_parts[3], CB: w_parts[2], GB: w_parts[3]}

        x_ring = sb("x_ring", [P, 2 * TB, D])
        v_hi = sb("v_hi", [P, 2 * TB, D], F32R)
        v_lo = sb("v_lo", [P, 2 * TB, D], F32R)
        wv_parts = [v[:, 0:C, :] for v in (v_hi, v_lo)]
        wo_parts = [v[:, C:2 * C, :] for v in (v_hi, v_lo)]
        pt_hi = sb("pt_hi", [P, TB, P], F32R)
        pt_lo = sb("pt_lo", [P, TB, P], F32R)
        h2_hi = sb("h2_hi", [P, C, P], F32R)
        h2_lo = sb("h2_lo", [P, C, P], F32R)
        x2n = sb("x2n", [P, D])
        attn = sb("attn", [P, D])
        ffn = sb("ffn", [P, D])
        f_hi = sb("f_hi", [P, C, D], F32R)
        f_lo = sb("f_lo", [P, C, D], F32R)
        probs = sb("probs", [P, KEYS])
        qs_hi = sb("qs_hi", [P, 2 * P], F32R)
        qs_lo = sb("qs_lo", [P, 2 * P], F32R)
        h2_f = sb("h2_f", [P, C, P])

        ps_s = bank("ps_s", KEYS)
        ps_t = [bank("ps_t0"), bank("ps_t1")]
        ps_v = bank("ps_v")
        ps_o = bank("ps_o")
        ps_y = bank("ps_y")
        ps_qk = bank("ps_qk")
        mod_banks = [ps_s[:, 0:D], ps_s[:, D:], ps_o[:], ps_y[:], ps_o[:], ps_y[:]]
        row_of = [0, 1, 2, 4, 5, 6]
        prologue_v = [ps_t[0], ps_v]
        mod_t_banks = [ps_t[0], ps_o]
        h2_parts_of = [(h2_hi, h2_lo), (h_hi[:, :, 0:P], h_lo[:, :, 0:P])]
        column_halves = [slice(0, D // 2), slice(D // 2, D)]
        last_banks = [ps_y, ps_o]
        wvo_banks = [ps_v, ps_o, ps_y, ps_qk]

        c_loaded, wqk_loaded, bias_loaded, f0_loaded = (
            sem(n) for n in ("c_loaded", "wqk_loaded", "bias_loaded", "f0_loaded"))
        wmod_loaded = [[sem(f"wmod_loaded{i}_{k}") for k in range(C)] for i in range(3)]
        wv_loaded = [sem(f"wv_loaded{k}") for k in range(C)]
        wo_loaded = [sem(f"wo_loaded{k}") for k in range(C)]
        f_added = [sem("f_added0"), sem("f_added1")]
        x_loaded = sem("x_loaded")
        y_stored = sem("y_stored")
        last_stored = sem("last_stored")
        last_steps = sem("last_steps")
        gate_stored = [sem("ga_stored"), sem("gb_stored")]
        gate_loaded = [sem("ga_loaded"), sem("gb_loaded")]
        consts_set = sem("consts_set")
        ident_set = sem("ident_set")
        silu_exp, silu_steps = sem("silu_exp"), sem("silu_steps")
        weights_hi_done, weights_lo_done = sem("weights_hi_done"), sem("weights_lo_done")
        w_hi_done = [None, sem("w_hi_done1"), sem("w_hi_done2")]
        w_lo_done = [None, sem("w_lo_done1"), sem("w_lo_done2")]
        mod_acc = sem("mod_acc")
        rows_done = sem("rows_done")
        mod_tps = sem("mod_tps")
        mod_t_done = sem("mod_t_done")
        wvo_acc, wvo_hi_done, wvo_lo_done = sem("wvo_acc"), sem("wvo_hi_done"), sem("wvo_lo_done")
        wqk_hi_done, wqk_lo_done = sem("wqk_hi_done"), sem("wqk_lo_done")
        f_hi_done, f_lo_done = sem("f_hi_done"), sem("f_lo_done")
        sp_passed, dve_passed, pool_passed = sem("sp_passed"), sem("dve_passed"), sem("pool_passed")
        stats1_done, mv1_done, ve1_done, rstd1_done, nmr1_done = (
            sem(n) for n in ("stats1_done", "mv1_done", "ve1_done", "rstd1_done", "nmr1_done"))
        xn_done, xt_ps, h_f_done, h_hi_done, h_lo_done = (
            sem(n) for n in ("xn_done", "xt_ps", "h_f_done", "h_hi_done", "h_lo_done"))
        v_acc, v_hi_done, v_lo_done = sem("v_acc"), sem("v_hi_done"), sem("v_lo_done")
        qk_acc, qk_hi_done, qk_lo_done, k_hi_done, k_lo_done = (
            sem(n) for n in ("qk_acc", "qk_hi_done", "qk_lo_done", "k_hi_done", "k_lo_done"))
        qs_hi_done, qs_lo_done = sem("qs_hi_done"), sem("qs_lo_done")
        s_acc, max_done, exp_done = sem("s_acc"), sem("max_done"), sem("exp_done")
        pt_ps, pt_hi_done, pt_lo_done, o_acc = (
            sem(n) for n in ("pt_ps", "pt_hi_done", "pt_lo_done", "o_acc"))
        rden_done, attn_done, x1_done = sem("rden_done"), sem("attn_done"), sem("x1_done")
        stats2_done, mv2_done, ve2_done, rstd2_done, nmr2_done = (
            sem(n) for n in ("stats2_done", "mv2_done", "ve2_done", "rstd2_done", "nmr2_done"))
        x2n_done, h2_ps, h2_f_done, h2_hi_done, h2_lo_done = (
            sem(n) for n in ("x2n_done", "h2_ps", "h2_f_done", "h2_hi_done", "h2_lo_done"))
        y_acc, ffn_done, gated_done, y_done = sem("y_acc"), sem("ffn_done"), sem("gated_done"), sem("y_done")

        def wait(eng, semaphore, value):
            if not isinstance(value, int) or value > 0:
                eng.wait_ge(semaphore, value)

        def wait_alone(eng, passed, semaphore, value):
            eng.wait_ge(semaphore, value)
            eng.sem_inc(passed, 1)

        def batch_of(pair):
            return (pair >> 2) & (B - 1)

        def full(ap):
            return ap.bitcast(F32)

        block = ctx.enter_context(nc.Block())

        @block.sync
        def _(sp):
            def load_x(pair):
                if not isinstance(pair, int) or pair > 0:
                    wait_alone(sp, sp_passed, x_loaded, pair * 16)
                slot = (pair & (2 * PB - 1)) * 2
                sp.dma_start(x_ring[:, bass.ds(slot, 2), :], x_pairs[pair]).then_inc(x_loaded, 16)

            def store_pair(pair):
                wait_alone(sp, sp_passed, y_done, 2 * pair + 2)
                if not isinstance(pair, int) or pair > 0:
                    wait_alone(sp, sp_passed, y_stored, pair * 16)
                slot = (pair & (2 * PB - 1)) * 2
                sp.dma_start(out_pairs[pair], x_ring[:, bass.ds(slot, 2), :]).then_inc(y_stored, 16)

            def load_rows(to, source, k, loaded):
                sp.dma_start(to[:, k, :], source[P * k:P * (k + 1), :]).then_inc(loaded[k], 16)

            def load_wmod(i):
                for k in range(C):
                    load_rows(wmod_sb[i], wmod[:, 2 * D * i:2 * D * (i + 1)], k, wmod_loaded[i])

            def spread_gate(i, vector):
                sp.dma_start(gate_rows[i], mod_rows[:, row_of[vector], :]).then_inc(gate_stored[i], 16)
                sp.wait_ge(gate_stored[i], 16)
                sp.dma_start(gates[:, i].rearrange("p b d -> p (b d)"), gate_rows[i].rearrange(
                    "b d -> (b d)").partition_broadcast(P)).then_inc(gate_loaded[i], 16)

            def load_v_and_o(k):
                load_rows(wv_raw, wv, k, wv_loaded)
                load_rows(wo_raw, wo_t, k, wo_loaded)

            sp.dma_start(c_sb[:].rearrange("p c b -> p (c b)"), c_t).then_inc(c_loaded, 16)
            load_wmod(0)
            load_v_and_o(0)
            load_x(0)
            for k in range(1, C):
                load_v_and_o(k)
            sp.dma_start(wqk_raw[:], wqk_t.rearrange("(c p) n -> p c n", p=P)).then_inc(wqk_loaded, 16)
            load_x(1)
            load_wmod(1)
            load_x(2)
            load_x(3)
            load_wmod(2)
            sp.wait_ge(w_lo_done[1], 2 * C)
            sp.dma_start(f_sum[:], factors[0].rearrange("(c p) n -> p c n", p=P)).then_inc(f0_loaded, 16)
            sp.wait_ge(mod_acc, SB + 1)
            load_x(4)
            load_x(5)
            sp.wait_ge(rows_done, ROWS_DONE[GA])
            sp.wait_ge(mod_tps, 1)
            spread_gate(0, GA)
            sp.dma_start(bias_bc[:], bias.partition_broadcast(P)).then_inc(bias_loaded, 16)
            sp.wait_ge(mod_acc, GB + 1)
            load_x(6)
            load_x(7)
            sp.wait_ge(rows_done, ROWS_DONE[GB])
            sp.wait_ge(mod_tps, 2)
            spread_gate(1, GB)

            def turn_over(pair):
                store_pair(pair)
                wait_alone(sp, sp_passed, y_stored, pair * 16 + 16)
                load_x(pair + 2 * PB)

            turn_over(0)
            with sp.Fori(1, PAIRS - 2 * PB) as pair:
                turn_over(pair)
            with sp.Fori(PAIRS - 2 * PB, PAIRS - 1) as pair:
                store_pair(pair)
            last = PAIRS - 1
            for half in range(2):
                sp.wait_ge(last_steps, 3 * half + 3)
                sp.dma_start(out_pairs[last][:, 1, column_halves[half]],
                             x_ring[:, 2 * TB - 1, column_halves[half]]).then_inc(last_stored, 16)
            sp.wait_ge(y_stored, last * 16)
            sp.wait_ge(last_stored, 48)

        @block.tensor
        def _(pe):
            def three(acc, a, b, first, last):
                (a_hi, a_lo), (b_hi, b_lo) = a, b
                nc.tensor.matmul(acc, a_hi, b_lo, start=first, stop=False)
                nc.tensor.matmul(acc, a_lo, b_hi, start=False, stop=False)
                return nc.tensor.matmul(acc, a_hi, b_hi, start=False, stop=last)

            def transposes(acc, source, n, base=0):
                for i in range(n):
                    last = nc.tensor.transpose(acc[:, P * i:P * (i + 1)],
                                               source[:, P * (base + i):P * (base + i + 1)], ident[:])
                return last

            def modulations(vectors):
                for k in range(C):
                    for v in vectors:
                        pe.wait_ge(wmod_loaded[v // 2][k], 16)
                        last = nc.tensor.matmul(mod_banks[v][0:B, :], silu_c[:, k, :],
                                                wmod_sb[v // 2][:, k, D * (v % 2):D * (v % 2 + 1)],
                                                start=(k == 0), stop=(k == C - 1))
                        if k == C - 1:
                            last.then_inc(mod_acc, 1)

            def modulations_by_parts(vectors):
                pe.wait_ge(silu_steps, 6)
                pe.wait_ge(w_lo_done[vectors[0] // 2], 2 * C)
                for v in vectors:
                    for k in range(C):
                        for part in (w_lo[v], w_hi[v]):
                            last = nc.tensor.matmul(mod_banks[v][0:LO_ROW + B, :], silu_parts[:, k, :], part[:, k, :],
                                                    start=(k == 0 and part is w_lo[v]),
                                                    stop=(k == C - 1 and part is w_hi[v]))
                    last.then_inc(mod_acc, 1)

            def modulation_columns(n, vectors):
                for i, v in enumerate(vectors):
                    for k in range(C):
                        at = (i * C + k) * B
                        last = nc.tensor.transpose(mod_t_banks[n][:, at:at + B], mod_rows[:, row_of[v], P * k:P * (k + 1)],
                                                   ident[0:B, 0:B])
                last.then_inc(mod_tps, 1)

            def transpose_x(q):
                pe.wait_ge(xn_done, q + 1)
                wait(pe, h_f_done, q)
                transposes(ps_t[1], xn, C).then_inc(xt_ps, 1)

            def project_values(q, u, acc=ps_v, banks=1):
                pe.wait_ge(h_lo_done, q + 1)
                wait(pe, v_lo_done, q + 1 - banks)
                for k in range(C):
                    if isinstance(q, int) and q == 0:
                        pe.wait_ge(wvo_lo_done, k + 1)
                    h = [part[:, k, P * u:P * (u + 1)] for part in (h_hi, h_lo)]
                    last = three(acc[:], h, (wvo_hi[:, k, :], wvo_lo[:, k, :]), k == 0, k == C - 1)
                last.then_inc(v_acc, 1)

            def project_qk(pair):
                wait(pe, qk_lo_done, pair)
                for k in range(C):
                    last = three(ps_qk[:, 0:2 * P], (wqk_hi[:, k, :], wqk_lo[:, k, :]),
                                 (h_hi[:, k, :], h_lo[:, k, :]), k == 0, k == C - 1)
                last.then_inc(qk_acc, 1)

            def scores(t, u, pair):
                pe.wait_ge(qs_hi_done, pair + 1)
                pe.wait_ge(qs_lo_done, pair + 1)
                pe.wait_ge(k_hi_done, (pair >> 2) * PB + PB)
                pe.wait_ge(k_lo_done, (pair >> 2) * PB + PB)
                wait(pe, exp_done, t)
                first = ((pair >> 2) & 1) * PB
                for n in range(2):
                    keys = k_both[:, bass.ds(first + 2 * n, 2), :]
                    acc = ps_s[:, D * n:D * (n + 1)]
                    nc.tensor.matmul(acc, qs_lo[:, P * u:P * (u + 1)], keys, start=True, stop=False)
                    last = nc.tensor.matmul(acc, qs_hi[:, P * u:P * (u + 1)], keys, start=False, stop=True)
                last.then_inc(s_acc, 1)

            def transpose_probs(t, prep):
                pe.wait_ge(exp_done, t + 1)
                wait(pe, h2_f_done, t - 1)
                transposes(ps_t[0], probs, HALF).then_inc(pt_ps, 1)
                if prep:
                    pe.wait_ge(h_f_done, t + TB + 1)
                wait(pe, pt_lo_done, 2 * t)
                transposes(ps_t[1], probs, HALF, HALF).then_inc(pt_ps, 1)

            def transpose_h2(t):
                pe.wait_ge(x2n_done, t + 1)
                pe.wait_ge(pt_lo_done, 2 * t + 3)
                transposes(ps_t[0], x2n, C).then_inc(h2_ps, 1)

            def attend(t, g, between=None):
                pe.wait_ge(v_lo_done, (g >> 2) * TB + TB)
                wait(pe, attn_done, t)
                first = ((g >> 2) & 1) * TB
                for j in range(TB):
                    if j % HALF == 0:
                        pe.wait_ge(pt_lo_done, 2 * t + 1 + j // HALF)
                    if j == HALF and between is not None:
                        transpose_h2(between)
                    v = [part[:, first + j, :] for part in (v_hi, v_lo)]
                    last = three(ps_o[:], (pt_hi[:, j, :], pt_lo[:, j, :]), v, j == 0, j == TB - 1)
                last.then_inc(o_acc, 1)

            def last_transpose():
                pe.wait_ge(x2n_done, T)
                pe.wait_ge(h2_f_done, T - 1)
                transposes(ps_t[0], x2n, C).then_inc(h2_ps, 1)

            def feed_forward(t, parts=h2_parts_of[0], acc=ps_y, between=None):
                pe.wait_ge(f_lo_done, C)
                pe.wait_ge(h2_lo_done, t + 1)
                if acc is ps_y:
                    wait(pe, ffn_done, t)
                for k in range(C):
                    if k == 2 and between is not None:
                        between()
                    last = three(acc[:], [part[:, k, :] for part in parts],
                                 (f_hi[:, k, :], f_lo[:, k, :]), k == 0, k == C - 1)
                last.then_inc(y_acc, 1)

            def prep_pair(pair, aside=None):
                for u in range(2):
                    transpose_x(2 * pair + u + 1)
                    if u:
                        pe.wait_ge(h_lo_done, 2 * pair + 2)
                        project_qk(pair)
                    if u and aside is not None:
                        aside()
                    project_values(2 * pair + u, u, prologue_v[u], 2)

            def step(g, u, prep=True, next_x=True, following=True, older=2, scores_early=False):
                t = 2 * g + u
                transpose_probs(t, prep)
                if older == 2:
                    feed_forward(t - 2)
                if prep:
                    if u:
                        pe.wait_ge(h_lo_done, t + TB + 1)
                        project_qk(g + PB)
                    if scores_early:
                        scores(t + 1, 1 - u, g + u)
                    project_values(t + TB, u)
                if following and not scores_early:
                    scores(t + 1, 1 - u, g + u)
                if next_x:
                    pe.wait_ge(pt_lo_done, 2 * t + 2)
                    transpose_x(t + TB + 1)
                if scores_early:
                    pe.wait_ge(mod_t_done, 4)
                attend(t, g, t - 1 if older else None)

            def project_weights(k):
                pe.wait_ge(weights_hi_done, 2 * k + 2)
                pe.wait_ge(weights_lo_done, 2 * k + 2)
                for m in range(C):
                    last = three(wvo_banks[m][:], [part[:, k, P * m:P * (m + 1)] for part in wv_parts],
                                 [part[:, k, :] for part in wo_parts], k == 0, k == C - 1)
                    if k == C - 1:
                        last.then_inc(wvo_acc, 1)

            def modulate_and_score():
                pe.wait_ge(rows_done, ROWS_DONE[GA])
                modulations_by_parts((CB,))
                pe.wait_ge(rows_done, ROWS_DONE[SB])
                modulations_by_parts((GB,))
                scores(0, 0, 0)

            pe.wait_ge(consts_set, 2)
            for _ in range(WARMUPS):
                nc.tensor.matmul(ps_t[0][0:LO_ROW + B, 0:C * (LO_ROW + B)], no_parts[:, 0, :],
                                 no_parts[:].rearrange("p c n -> p (c n)"), start=True, stop=True)
            pe.wait_ge(silu_steps, 3)
            modulations((SA, CA))
            project_weights(0)
            pe.wait_ge(ident_set, 2)
            transpose_x(0)
            pe.wait_ge(rows_done, 2)
            modulation_columns(0, (SA, CA))
            for k in range(1, C):
                project_weights(k)
            pe.wait_ge(wqk_lo_done, 1)
            prep_pair(0)
            modulations_by_parts((GA, SB))
            with pe.Fori(1, PB - 1) as pair:
                prep_pair(pair)
            prep_pair(PB - 1, modulate_and_score)
            pe.wait_ge(rows_done, ROWS_DONE[CB])
            modulation_columns(1, (SB, CB))
            pe.wait_ge(v_lo_done, TB - 1)
            step(0, 0, older=0, scores_early=True)
            step(0, 1, older=1)
            pe.wait_ge(rows_done, ROWS_DONE[GB])
            with pe.Fori(1, PAIRS - PB - 1) as g:
                for u in range(2):
                    step(g, u)
            step(PAIRS - PB - 1, 0)
            step(PAIRS - PB - 1, 1, next_x=False)
            with pe.Fori(PAIRS - PB, PAIRS - 1) as g:
                for u in range(2):
                    step(g, u, prep=False, next_x=False)
            step(PAIRS - 1, 0, prep=False, next_x=False)
            transpose_probs(T - 1, False)
            attend(T - 1, PAIRS - 1)
            pe.wait_ge(x2n_done, T - 1)
            transposes(ps_t[0], x2n, C).then_inc(h2_ps, 1)
            feed_forward(T - 3)
            feed_forward(T - 2, h2_parts_of[1], ps_v, last_transpose)
            pe.wait_ge(ffn_done, T - 2)
            for half, bank_ in enumerate(last_banks):
                for k in range(C):
                    if half == 0:
                        pe.wait_ge(h2_lo_done, T + k)
                    last = three(bank_[:, 0:D // 2], (h2_hi[:, k, :], h2_lo[:, k, :]),
                                 [part[:, k, column_halves[half]] for part in (f_hi, f_lo)], k == 0, k == C - 1)
                last.then_inc(y_acc, 1)

        @block.scalar
        def _(act):
            def rounded(to, source):
                return nc.scalar.activation(to, source, ACT.Identity)

            def modulate(to, source, b, v):
                for k in range(C):
                    last = nc.scalar.activation(to[:, k, :], source[:, P * k:P * (k + 1)], ACT.Identity,
                                                scale=mod_t[:, b, v + 1, k:k + 1], bias=mod_t[:, b, v, k:k + 1])
                return last

            def normalize_x(q, u):
                act.wait_ge(nmr1_done, q + 1)
                wait(act, xt_ps, q)
                nc.scalar.activation(xn[:], x_ring[:, q & (2 * TB - 1), :], ACT.Identity,
                                     scale=rstd1[:, u:u + 1], bias=nmr1[:, u:u + 1]).then_inc(xn_done, 1)

            def modulate_x(q, b):
                act.wait_ge(xt_ps, q + 1)
                wait(act, h_lo_done, q)
                modulate(h_f, ps_t[1], b, 0).then_inc(h_f_done, 1)

            def values(q, acc=ps_v):
                act.wait_ge(v_acc, q + 1)
                rounded(v_hi[:, q & (2 * TB - 1), :], acc[:]).then_inc(v_hi_done, 1)

            def qk(pair):
                act.wait_ge(qk_acc, pair + 1)
                rounded(qk_hi[:, pair & (PB - 1), :], ps_qk[:, 0:2 * P]).then_inc(qk_hi_done, 1)
                rounded(k_both[0:R, pair & (2 * PB - 1), :], ps_qk[R:2 * R, 0:2 * P]).then_inc(k_hi_done, 1)

            def pair_q(pair):
                act.wait_ge(qk_hi_done, pair + 1)
                wait(act, s_acc, 2 * pair)
                source = full(qk_hi[0:R, pair & (PB - 1), :])
                rounded(qs_hi[0:R, :], source)
                rounded(qs_hi[R:2 * R, :], source).then_inc(qs_hi_done, 1)

            def exponentials(t, u):
                act.wait_ge(max_done, t + 1)
                nc.scalar.activation(probs[:], ps_s[:], ACT.Exp, bias=negmax[:, u:u + 1],
                                     accum_out=rowsum[:, u:u + 1]).then_inc(exp_done, 1)

            def probs_parts(t):
                for half in range(2):
                    act.wait_ge(pt_ps, 2 * t + half + 1)
                    rounded(pt_hi[:, HALF * half:HALF * (half + 1), :],
                            ps_t[half][:]).then_inc(pt_hi_done, 1)

            def normalize_x1(t, u):
                act.wait_ge(nmr2_done, t + 1)
                wait(act, h2_ps, t)
                nc.scalar.activation(x2n[:], x_ring[:, t & (2 * TB - 1), :], ACT.Identity,
                                     scale=rstd2[:, u:u + 1], bias=nmr2[:, u:u + 1]).then_inc(x2n_done, 1)

            def modulate_x1(t, b):
                act.wait_ge(h2_ps, t + 1)
                wait(act, h2_lo_done, t)
                modulate(h2_f, ps_t[0], b, 2).then_inc(h2_f_done, 1)

            def factor_parts():
                for half in range(2):
                    act.wait_ge(f_added[half], 16 * (NF - 1))
                for k in range(C):
                    rounded(f_hi[:, k, :], f_sum[:, k, :]).then_inc(f_hi_done, 1)

            def step(g, u, prep=True, next_x=True, next_norm=True, following=True, older=2, last_pair=False,
                     aside=None):
                t = 2 * g + u
                probs_parts(t)
                if prep and u:
                    qk(g + PB)
                if older:
                    normalize_x1(t - 1, 1 - u)
                if prep:
                    values(t + TB)
                if next_x:
                    modulate_x(t + TB + 1, batch_of(g + u + PB))
                if aside is not None:
                    aside()
                if following:
                    exponentials(t + 1, 1 - u)
                    if u == 0 and not last_pair:
                        pair_q(g + 1)
                if older:
                    modulate_x1(t - 1, batch_of(g - 1 + u))
                if next_norm:
                    normalize_x(t + TB + 2, u)

            def weight_parts(k):
                act.wait_ge(wv_loaded[k], 16)
                rounded(wv_parts[0][:, k, :], wv_raw[:, k, :]).then_inc(weights_hi_done, 1)
                act.wait_ge(wo_loaded[k], 16)
                rounded(wo_parts[0][:, k, :], wo_raw[:, k, :]).then_inc(weights_hi_done, 1)

            def wmod_parts(v, k):
                source = wmod_sb[v // 2][:, k, D * (v % 2):D * (v % 2 + 1)]
                rounded(w_hi[v][:, k, :], source).then_inc(w_hi_done[v // 2], 1)

            def first_wmod_parts(k):
                act.wait_ge(wmod_loaded[1][k], 16)
                wmod_parts(GA, k)
                wmod_parts(SB, k)

            def prep_pair(pair, first_scores=False, aside=None):
                for u in range(2):
                    q = 2 * pair + u
                    if u:
                        qk(pair)
                        if first_scores:
                            pair_q(0)
                    modulate_x(q + 1, batch_of(pair + u))
                    normalize_x(q + 2, u)
                    if aside is not None:
                        aside(q)
                    if u and first_scores:
                        exponentials(0, 0)
                    values(q, prologue_v[u])

            act.wait_ge(c_loaded, 16)
            nc.scalar.activation(silu_den[:], c_sb[:], ACT.Exp, scale=-1.0).then_inc(silu_exp, 1)
            weight_parts(0)
            weight_parts(1)
            normalize_x(0, 0)
            weight_parts(2)
            weight_parts(3)
            act.wait_ge(mod_t_done, 2)
            modulate_x(0, 0)
            normalize_x(1, 1)
            act.wait_ge(wqk_loaded, 16)
            rounded(wqk_hi[:], wqk_raw[:]).then_inc(wqk_hi_done, 1)
            for k in range(C - 1):
                first_wmod_parts(k)
            for m in range(C):
                act.wait_ge(wvo_acc, m + 1)
                rounded(wvo_hi[:, m, :], wvo_banks[m][:]).then_inc(wvo_hi_done, 1)
            prep_pair(0, aside=lambda q: first_wmod_parts(C - 1) if q == 0 else None)
            for k in range(C):
                act.wait_ge(wmod_loaded[2][k], 16)
                wmod_parts(CB, k)
            act.wait_ge(mod_acc, SB + 1)
            with act.Fori(1, PB - 1) as pair:
                prep_pair(pair, aside=lambda q: wmod_parts(GB, q - 2))
            prep_pair(PB - 1, first_scores=True)
            step(0, 0, older=0)
            act.wait_ge(mod_t_done, 4)
            step(0, 1, older=1, aside=factor_parts)
            with act.Fori(1, PAIRS - PB - 1) as g:
                for u in range(2):
                    step(g, u)
            step(PAIRS - PB - 1, 0, next_norm=False)
            step(PAIRS - PB - 1, 1, next_x=False, next_norm=False)
            with act.Fori(PAIRS - PB, PAIRS - 1) as g:
                for u in range(2):
                    step(g, u, prep=False, next_x=False, next_norm=False)
            step(PAIRS - 1, 0, prep=False, next_x=False, next_norm=False, last_pair=True)
            step(PAIRS - 1, 1, prep=False, next_x=False, next_norm=False, following=False)
            normalize_x1(T - 1, 1)
            act.wait_ge(h2_ps, T)
            act.wait_ge(h2_lo_done, T - 1)
            for k in range(C):
                nc.scalar.activation(h2_f[:, k, :], ps_t[0][:, P * k:P * (k + 1)], ACT.Identity,
                                     scale=mod_t[:, B - 1, 3, k:k + 1],
                                     bias=mod_t[:, B - 1, 2, k:k + 1]).then_inc(h2_f_done, 1)
            act.wait_ge(y_done, T - 1)
            act.dma_start(out_pairs[PAIRS - 1][:, 0], x_ring[:, 2 * TB - 2, :]).then_inc(last_stored, 16)

        @block.vector
        def _(dve):
            def rest(to, whole, hi):
                return nc.vector.tensor_tensor(to, whole, full(hi), ALU.subtract)

            def x_stats(q, u):
                nc.vector.bn_stats(stats1[:, u, :], x_ring[:, q & (2 * TB - 1), :]).then_inc(stats1_done, 1)
                wait_alone(dve, dve_passed, stats1_done, q + 1)
                nc.vector.bn_aggr(mv1[:, u, :], stats1[:, u, :]).then_inc(mv1_done, 1)

            def h_parts(q, pair, u):
                dve.wait_ge(h_f_done, q + 1)
                wait(dve, qk_acc, pair)
                here = slice(P * u, P * (u + 1))
                nc.vector.tensor_copy(h_hi[:, :, here], h_f[:]).then_inc(h_hi_done, 1)
                dve.wait_ge(h_hi_done, q + 1)
                rest(h_lo[:, :, here], h_f[:], h_hi[:, :, here]).then_inc(h_lo_done, 1)

            def values(q, acc=ps_v):
                dve.wait_ge(v_hi_done, q + 1)
                slot = q & (2 * TB - 1)
                rest(v_lo[:, slot, :], acc[:], v_hi[:, slot, :]).then_inc(v_lo_done, 1)

            def qk(pair):
                dve.wait_ge(qk_hi_done, pair + 1)
                slot = pair & (PB - 1)
                dve.wait_ge(k_hi_done, pair + 1)
                rest(qk_lo[:, slot, :], ps_qk[:, 0:2 * P], qk_hi[:, slot, :]).then_inc(qk_lo_done, 1)
                dve.wait_ge(qk_lo_done, pair + 1)
                nc.vector.tensor_copy(k_both[R:2 * R, pair & (2 * PB - 1), :],
                                      full(qk_lo[R:2 * R, slot, :])).then_inc(k_lo_done, 1)

            def pair_q(pair):
                dve.wait_ge(qk_lo_done, pair + 1)
                wait(dve, s_acc, 2 * pair)
                source = full(qk_lo[0:R, pair & (PB - 1), :])
                nc.vector.tensor_copy(qs_lo[0:R, :], source)
                nc.vector.tensor_copy(qs_lo[R:2 * R, :], source).then_inc(qs_lo_done, 1)

            def row_max(t, u):
                dve.wait_ge(s_acc, t + 1)
                nc.vector.tensor_reduce(negmax[:, u:u + 1], ps_s[:], AX_X, ALU.max,
                                        negate=True).then_inc(max_done, 1)

            def probs_rest(t, half):
                dve.wait_ge(pt_hi_done, 2 * t + half + 1)
                here = slice(HALF * half, HALF * (half + 1))
                rest(pt_lo[:, here, :], ps_t[half][:].rearrange("p (j i) -> p j i", i=P),
                     pt_hi[:, here, :]).then_inc(pt_lo_done, 1)

            def h2_parts(t, chunks=slice(0, C), done=0, to=h2_parts_of[0]):
                hi, lo = [part[:, chunks, :] for part in to]
                source = h2_f[:, chunks, :]
                dve.wait_ge(h2_f_done, t + done + 1)
                nc.vector.tensor_copy(hi, source).then_inc(h2_hi_done, 1)
                dve.wait_ge(h2_hi_done, t + done + 1)
                rest(lo, source, hi).then_inc(h2_lo_done, 1)

            def gate_attention(t, u, b):
                dve.wait_ge(exp_done, t + 1)
                nc.vector.reciprocal(rden[:, u:u + 1], rowsum[:, u:u + 1]).then_inc(rden_done, 1)
                dve.wait_ge(o_acc, t + 1)
                dve.wait_ge(rden_done, t + 1)
                nc.vector.scalar_tensor_tensor(out=attn[:], in0=ps_o[:], scalar=rden[:, u:u + 1],
                                               in1=gates[:, 0, b, :], op0=ALU.mult,
                                               op1=ALU.mult).then_inc(attn_done, 1)

            def add_x(t):
                dve.wait_ge(attn_done, t + 1)
                tile = x_ring[:, t & (2 * TB - 1), :]
                nc.vector.tensor_tensor(tile, attn[:], tile, ALU.add).then_inc(x1_done, 1)

            def x1_stats(t, u):
                tile = x_ring[:, t & (2 * TB - 1), :]
                wait_alone(dve, dve_passed, x1_done, t + 1)
                nc.vector.bn_stats(stats2[:, u, :], tile).then_inc(stats2_done, 1)
                wait_alone(dve, dve_passed, stats2_done, t + 1)
                nc.vector.bn_aggr(mv2[:, u, :], stats2[:, u, :]).then_inc(mv2_done, 1)

            def factor_rests():
                for k in range(C // 2):
                    dve.wait_ge(f_hi_done, k + 1)
                    rest(f_lo[:, k, :], f_sum[:, k, :], f_hi[:, k, :]).then_inc(f_lo_done, 1)

            def ffn_out(t, acc=ps_y, to=ffn):
                dve.wait_ge(y_acc, t + 1)
                if to is ffn:
                    wait(dve, y_done, t)
                nc.vector.scalar_tensor_tensor(out=to[:, 0:D], in0=acc[:], scalar=FSCALE, in1=bias_bc[:],
                                               op0=ALU.mult, op1=ALU.add).then_inc(ffn_done, 1)

            def step(g, u, prep=True, next_x=True, next_norm=True, following=True, older=2, last_pair=False,
                     early=None, late=None):
                t = 2 * g + u
                probs_rest(t, 0)
                if older:
                    x1_stats(t - 1, 1 - u)
                probs_rest(t, 1)
                if older == 2:
                    ffn_out(t - 2)
                if prep:
                    if u:
                        qk(g + PB)
                    if early is not None:
                        early()
                    values(t + TB)
                if following:
                    row_max(t + 1, 1 - u)
                    if u == 0 and not last_pair:
                        pair_q(g + 1)
                if next_norm:
                    if u == 0:
                        wait_alone(dve, dve_passed, x_loaded, 16 * (g + PB + 2))
                    x_stats(t + TB + 2, u)
                if next_x:
                    h_parts(t + TB + 1, g + u + PB, 1 - u)
                if late is not None:
                    late()
                if older:
                    h2_parts(t - 1)
                gate_attention(t, u, batch_of(g))
                if not (last_pair and u == 0):
                    add_x(t)

            def weight_rests(k):
                for i, (parts, raw) in enumerate(((wv_parts, wv_raw), (wo_parts, wo_raw))):
                    dve.wait_ge(weights_hi_done, 2 * k + i + 1)
                    rest(parts[1][:, k, :], raw[:, k, :], parts[0][:, k, :]).then_inc(weights_lo_done, 1)

            def last_vector_rest(k):
                dve.wait_ge(w_hi_done[2], C + 1 + k)
                rest(w_lo[GB][:, k, :], wmod_2[:, k, D:], w_hi[GB][:, k, :]).then_inc(w_lo_done[2], 1)

            def prep_pair(pair, between=None, first_scores=None, aside=None):
                for u in range(2):
                    q = 2 * pair + u
                    if u:
                        if between is not None:
                            between()
                        qk(pair)
                        if first_scores is not None:
                            pair_q(0)
                    h_parts(q + 1, pair + u, 1 - u)
                    if u and first_scores is not None:
                        first_scores()
                    else:
                        if u:
                            wait_alone(dve, dve_passed, x_loaded, 16 * (pair + 3))
                        x_stats(q + 3, 1 - u)
                    values(q, prologue_v[u])
                    if aside is not None:
                        aside(q)

            nc.vector.memset(minus_half[:], -0.5).then_inc(consts_set, 1)
            nc.vector.memset(no_parts[:], 0.0).then_inc(consts_set, 1)
            dve.wait_ge(silu_exp, 1)
            nc.vector.tensor_scalar(silu_den[:], silu_den[:], 1.0, None, ALU.add).then_inc(silu_steps, 1)
            dve.wait_ge(silu_steps, 1)
            nc.vector.reciprocal(silu_den[:], silu_den[:]).then_inc(silu_steps, 1)
            dve.wait_ge(silu_steps, 2)
            nc.vector.tensor_tensor(silu_c[:], c_sb[:], silu_den[:], ALU.mult).then_inc(silu_steps, 1)
            dve.wait_ge(consts_set, 2)
            nc.vector.tensor_copy(silu_parts[:], no_parts[:]).then_inc(silu_steps, 1)
            dve.wait_ge(silu_steps, 4)
            nc.vector.tensor_copy(silu_parts[:, :, 0:B], silu_c[:]).then_inc(silu_steps, 1)
            dve.wait_ge(silu_steps, 5)
            rest(silu_parts[:, :, LO_ROW:], silu_c[:], silu_parts[:, :, 0:B]).then_inc(silu_steps, 1)
            rows = [0]

            def row(v):
                dve.wait_ge(mod_acc, v + 1)
                acc, to = mod_banks[v][0:B, :], mod_rows[:, row_of[v], :]
                if v in w_hi:
                    low = mod_rows[:, row_of[GB] + 1, :]
                    dve.wait_ge(rows_done, rows[0])
                    nc.vector.tensor_copy(low, mod_banks[v][LO_ROW:LO_ROW + B, :]).then_inc(rows_done, 1)
                    dve.wait_ge(rows_done, rows[0] + 1)
                    nc.vector.tensor_tensor(to, acc, low, ALU.add).then_inc(rows_done, 1)
                    rows[0] += 2
                else:
                    nc.vector.tensor_copy(to, acc).then_inc(rows_done, 1)
                    rows[0] += 1

            def gate_row(v):
                row(v)
                gate, sign = mod_rows[:, row_of[v], :], mod_rows[:, row_of[v] + 1, :]
                dve.wait_ge(rows_done, rows[0])
                nc.vector.tensor_scalar(sign, gate, 0.0, 2.0, ALU.is_ge, ALU.mult).then_inc(rows_done, 1)
                dve.wait_ge(rows_done, rows[0] + 1)
                nc.vector.tensor_scalar(sign, sign, -1.0, None, ALU.add).then_inc(rows_done, 1)
                dve.wait_ge(rows_done, rows[0] + 2)
                nc.vector.tensor_tensor(gate, gate, sign, ALU.mult).then_inc(rows_done, 1)
                dve.wait_ge(rows_done, rows[0] + 3)
                nc.vector.scalar_tensor_tensor(out=gate, in0=gate, scalar=GATE_FLOOR, in1=sign,
                                               op0=ALU.max, op1=ALU.mult).then_inc(rows_done, 1)
                rows[0] += 4

            def columns(n):
                dve.wait_ge(mod_tps, n + 1)
                for i in range(2):
                    source = mod_t_banks[n][:, i * C * B:(i + 1) * C * B].rearrange("p (c b) -> p b c", b=B)
                    nc.vector.tensor_scalar(mod_t[:, :, 2 * n + i, :], source, float(i), None,
                                            ALU.add).then_inc(mod_t_done, 1)

            def first_scores_max():
                row(CB)
                row_max(0, 0)

            weight_rests(0)
            dve.wait_ge(x_loaded, 16)
            x_stats(0, 0)
            x_stats(1, 1)
            weight_rests(1)
            row(SA)
            row(CA)
            columns(0)
            weight_rests(2)
            weight_rests(3)
            dve.wait_ge(wqk_hi_done, 1)
            rest(wqk_lo[:], wqk_raw[:], wqk_hi[:]).then_inc(wqk_lo_done, 1)
            h_parts(0, 0, 0)
            dve.wait_ge(x_loaded, 32)
            x_stats(2, 0)
            for v in (GA, SB):
                dve.wait_ge(w_hi_done[1], v - GA + 3)
                rest(w_lo[v][:, 1, :], wmod_sb[1][:, 1, D * (v % 2):D * (v % 2 + 1)],
                     w_hi[v][:, 1, :]).then_inc(w_lo_done[1], 1)
            for m in range(C):
                dve.wait_ge(wvo_hi_done, m + 1)
                rest(wvo_lo[:, m, :], wvo_banks[m][:], wvo_hi[:, m, :]).then_inc(wvo_lo_done, 1)
            prep_pair(0)
            gate_row(GA)
            with dve.Fori(1, PB - 1) as pair:
                prep_pair(pair, aside=lambda q: last_vector_rest(q - 2))
            prep_pair(PB - 1, lambda: row(SB), first_scores_max)
            columns(1)
            dve.wait_ge(gate_loaded[0], 16)
            dve.wait_ge(bias_loaded, 16)
            step(0, 0, older=0, early=lambda: gate_row(GB))
            step(0, 1, older=1, late=factor_rests)
            with dve.Fori(1, PAIRS - PB - 1) as g:
                for u in range(2):
                    step(g, u)
            step(PAIRS - PB - 1, 0, next_norm=False)
            step(PAIRS - PB - 1, 1, next_x=False, next_norm=False)
            with dve.Fori(PAIRS - PB, PAIRS - 1) as g:
                for u in range(2):
                    step(g, u, prep=False, next_x=False, next_norm=False)
            step(PAIRS - 1, 0, prep=False, next_x=False, next_norm=False, last_pair=True)
            probs_rest(T - 1, 0)
            add_x(T - 2)
            x1_stats(T - 2, 0)
            probs_rest(T - 1, 1)
            gate_attention(T - 1, 1, B - 1)
            add_x(T - 1)
            x1_stats(T - 1, 1)
            h2_parts(T - 2, to=h2_parts_of[1])
            ffn_out(T - 3)
            for k in range(C):
                h2_parts(T - 1, slice(k, k + 1), k)
            ffn_out(T - 2, ps_v, probs)
            for half, columns_ in enumerate(column_halves):
                y, tile = attn[:, columns_], x_ring[:, 2 * TB - 1, columns_]
                dve.wait_ge(y_acc, T + half)
                nc.vector.scalar_tensor_tensor(out=y, in0=last_banks[half][:, 0:D // 2], scalar=FSCALE,
                                               in1=bias_bc[:, columns_], op0=ALU.mult,
                                               op1=ALU.add).then_inc(last_steps, 1)
                dve.wait_ge(last_steps, 3 * half + 1)
                nc.vector.tensor_tensor(y, y, gates[:, 1, B - 1, columns_], ALU.mult).then_inc(last_steps, 1)
                dve.wait_ge(last_steps, 3 * half + 2)
                nc.vector.tensor_tensor(tile, y, tile, ALU.add).then_inc(last_steps, 1)

        @block.gpsimd
        def _(pool):
            def inverse_std(count, u, mv, ve, rstd, nmr, mv_done, ve_done, rstd_done, nmr_done):
                wait_alone(pool, pool_passed, mv_done, count)
                one = slice(u, u + 1)
                nc.gpsimd.tensor_scalar(ve[:, one], mv[:, u, 1:2], EPS, None, ALU.add).then_inc(ve_done, 1)
                pool.wait_ge(ve_done, count)
                nc.gpsimd.tensor_tensor(rstd[:, one], ve[:, one], minus_half[:], ALU.pow).then_inc(rstd_done, 1)
                wait_alone(pool, pool_passed, rstd_done, count)
                nc.gpsimd.tensor_scalar(nmr[:, one], mv[:, u, 0:1], rstd[:, one], -1.0,
                                        ALU.mult, ALU.mult).then_inc(nmr_done, 1)

            def of_x(q, u):
                inverse_std(q + 1, u, mv1, ve1, rstd1, nmr1, mv1_done, ve1_done, rstd1_done, nmr1_done)

            def of_x1(t, u):
                inverse_std(t + 1, u, mv2, ve2, rstd2, nmr2, mv2_done, ve2_done, rstd2_done, nmr2_done)

            def result(t, b, ffn=ffn):
                wait_alone(pool, pool_passed, ffn_done, t + 1)
                nc.gpsimd.tensor_tensor(ffn[:, 0:D], ffn[:, 0:D], gates[:, 1, b, :], ALU.mult).then_inc(gated_done, 1)
                wait_alone(pool, pool_passed, gated_done, t + 1)
                tile = x_ring[:, t & (2 * TB - 1), :]
                nc.gpsimd.tensor_tensor(tile, ffn[:, 0:D], tile, ALU.add).then_inc(y_done, 1)

            def step(g, u, next_norm=True):
                t = 2 * g + u
                result(t - 2, batch_of(g - 1))
                if next_norm:
                    of_x(t + TB + 2, u)
                of_x1(t, u)

            nc.gpsimd.memset(ident[:], 0.0).then_inc(ident_set, 1)
            pool.wait_ge(ident_set, 1)
            nc.gpsimd.affine_select(out=ident[:], in_=ident[:], compare_op=ALU.not_equal, fill=1.0, base=0,
                                    pattern=[[-1, P]], channel_multiplier=1).then_inc(ident_set, 1)
            pool.wait_ge(consts_set, 1)
            of_x(0, 0)
            of_x(1, 1)

            def add_half(i, half):
                if i == 1:
                    pool.wait_ge(f0_loaded, 16)
                wait(pool, f_added[half], 16 * (i - 1))
                rows = slice(D // 2 * half, D // 2 * (half + 1))
                nc.gpsimd.dma_start(f_sum[:, C // 2 * half:C // 2 * (half + 1), :],
                                    factors[i][rows, :].rearrange("(c p) n -> p c n", p=P),
                                    accum_op=ALU.add).then_inc(f_added[half], 16)

            def add_factor(i):
                add_half(i, 0)
                add_half(i, 1)

            def wmod_rest(v, k, count):
                pool.wait_ge(w_hi_done[v // 2], count)
                nc.gpsimd.tensor_tensor(w_lo[v][:, k, :], wmod_sb[v // 2][:, k, D * (v % 2):D * (v % 2 + 1)],
                                        full(w_hi[v][:, k, :]), ALU.subtract).then_inc(w_lo_done[v // 2], 1)

            def first_rests(k):
                wmod_rest(GA, k, 2 * k + 1)
                wmod_rest(SB, k, 2 * k + 2)

            first_rests(0)
            of_x(2, 0)
            first_rests(2)
            first_rests(3)
            of_x(3, 1)
            of_x(4, 0)
            add_factor(1)
            pool.wait_ge(mod_acc, SB + 1)
            for k in range(C):
                if k:
                    of_x(4 + k, k % 2)
                wmod_rest(CB, k, k + 1)
                if k:
                    add_half(2 + (k - 1) // 2, (k - 1) % 2)
            of_x(TB, 0)
            add_half(3, 1)
            add_factor(4)
            of_x(TB + 1, 1)
            add_factor(5)
            add_factor(6)
            of_x(TB + 2, 0)
            add_factor(7)
            of_x1(0, 0)
            of_x(TB + 3, 1)
            for k in range(C // 2, C):
                pool.wait_ge(f_hi_done, k + 1)
                nc.gpsimd.tensor_tensor(f_lo[:, k, :], f_sum[:, k, :], full(f_hi[:, k, :]),
                                        ALU.subtract).then_inc(f_lo_done, 1)
            of_x1(1, 1)
            pool.wait_ge(gate_loaded[1], 16)
            with pool.Fori(1, PAIRS - PB - 1) as g:
                for u in range(2):
                    step(g, u)
            with pool.Fori(PAIRS - PB - 1, PAIRS - 1) as g:
                for u in range(2):
                    step(g, u, next_norm=False)
            step(PAIRS - 1, 0, next_norm=False)
            of_x1(T - 1, 1)
            result(T - 3, B - 1)
            result(T - 2, B - 1, probs)


_NAMES = ["x", "wqk_t", "wv", "wo_t", "factors", "bias", "c_t", "wmod"]


def kernel(L0_attn_hidden_states, L0_attn_Wq, L0_attn_Wk, L0_attn_Wv, L0_attn_Wo, L0_ffn_factors,
           L0_ffn_bias, L0_c, L0_wmod):
    import numpy as np
    import concourse.bacc as bacc
    from concourse.bass_utils import run_bass_kernel_spmd

    hidden = np.asarray(L0_attn_hidden_states)
    batch, seq, dim = hidden.shape
    c = np.asarray(L0_c)
    laid_out = [
        hidden.reshape(batch * seq, dim),
        np.concatenate([np.asarray(L0_attn_Wq), np.asarray(L0_attn_Wk)]).T,
        np.asarray(L0_attn_Wv),
        np.asarray(L0_attn_Wo).T,
        np.asarray(L0_ffn_factors),
        np.asarray(L0_ffn_bias),
        c.T.reshape(dim // P, P, batch).transpose(1, 0, 2).reshape(P, -1),
        np.asarray(L0_wmod),
    ]
    nc = bacc.Bacc("TRN2", target_bir_lowering=False, num_devices=1)
    arrays, args = {}, []
    for name, a in zip(_NAMES, laid_out):
        arrays[f"in_{name}"] = np.ascontiguousarray(a)
        args.append(nc.dram_tensor(f"in_{name}", a.shape, mybir.dt.from_np(a.dtype), kind="ExternalInput").ap())
    args.append(nc.dram_tensor("result", (batch * seq, dim), F32, kind="ExternalOutput").ap())
    adaln_block(nc, *args)
    r = run_bass_kernel_spmd(nc, [arrays], core_ids=[0])
    return r.results[0]["result"].reshape(batch, seq, dim)
```
